# Optimizing a Trainium2 kernel written in Bass

```python
import numpy as np
import jax
import jax.numpy as jnp

def _softmax(x, axis=-1):
    return jax.nn.softmax(x, axis=axis)

def _gelu(x):
    return jax.nn.gelu(x, approximate=True)

def _silu(x):
    return jax.nn.silu(x)

def _sigmoid(x):
    return jax.nn.sigmoid(x)

def _layernorm(x, axis=-1, eps=1e-05):
    m = jnp.mean(x, axis=axis, keepdims=True)
    v = jnp.var(x, axis=axis, keepdims=True)
    return (x - m) / jnp.sqrt(v + eps)

def _scatter_add(tgt, idx, src, axis=0):
    return tgt.at[idx].add(src)

def _segment_sum(src, seg, n):
    return jax.ops.segment_sum(src, seg, n)
kernel_name = 'mk_xattn_ffn_d1_seqx_r8_e41e6f'

def setup_inputs(seed: int=0):
    np.random.seed(seed)
    _w = jnp.asarray

    def _rec_inputs():
        import jax
        import jax.numpy as jnp
        _rk = jax.random.key(seed)
        x = 7.22e-05 + 1 * jax.random.normal(jax.random.fold_in(_rk, 1), (32, 64, 256), jnp.float32)
        _lenS = 64 - jax.random.randint(jax.random.fold_in(_rk, 7), (32,), 0, max(1, 64 // 4) + 1, jnp.int32)
        _lenS2 = 64 - jax.random.randint(jax.random.fold_in(_rk, 8), (32,), 0, max(1, 64 // 4) + 1, jnp.int32)
        _ctx_2048P = jax.random.normal(jax.random.fold_in(_rk, 11), (32, 16, 256), jnp.float32)
        _ctx_2048c = jax.random.dirichlet(jax.random.fold_in(_rk, 511), 0.3 * jnp.ones((16,), jnp.float32), (32, 64))
        _ctx_2048t = jnp.einsum('bsk,bkd->bsd', _ctx_2048c, _ctx_2048P)
        _ctx_2048t = _ctx_2048t * jax.lax.rsqrt(jnp.mean(jnp.square(_ctx_2048t)) + 1e-12) * 0.953939
        ctx_2048 = 4.13588e-05 + 0.999923 * (_ctx_2048t + 0.3 * jax.random.normal(jax.random.fold_in(_rk, 611), (32, 64, 256), jnp.float32))
        return (x, ctx_2048)
    x, ctx_2048 = _rec_inputs()

    def _L0_xattn_setup():
        import jax, jax.numpy as jnp
        import numpy as np
        N_HEAD = 8
        key = jax.random.key(seed)
        k1, k2, k3 = jax.random.split(key, 3)
        b, d, m = (4, 128, 256)
        c, n = (128, 256)
        q = jax.random.normal(k1, (b, d, m), dtype=jnp.float32)
        k = jax.random.normal(k2, (d // d * b, d, n), dtype=jnp.float32).reshape(b, d, n)
        v = jax.random.normal(k3, (b, c, n), dtype=jnp.float32)
        return {'q': q, 'k': k, 'v': v}
    _L0_xattn_all = _L0_xattn_setup()
    _L0_xattn_in = {k: v for k, v in _L0_xattn_all.items() if k in ()}
    del _L0_xattn_all

    def _L0_ffn_setup():
        import jax, jax.numpy as jnp
        import numpy as np
        NUM_EXPERTS = 8
        TOP_K = 2
        EMB = 256
        MLP = 512
        B, S = (4, 128)
        key = jax.random.key(seed)
        ks = jax.random.split(key, 5)
        scale_x = 1.0
        return {'x': jax.random.normal(ks[0], (B, S, EMB), dtype=jnp.float32), 'gate_kernel': jax.random.normal(ks[1], (EMB, NUM_EXPERTS), dtype=jnp.float32) / np.sqrt(EMB), 'w0_kernel': jax.random.normal(ks[2], (NUM_EXPERTS, EMB, MLP), dtype=jnp.float32) / np.sqrt(EMB), 'w1_kernel': jax.random.normal(ks[3], (NUM_EXPERTS, EMB, MLP), dtype=jnp.float32) / np.sqrt(EMB), 'wo_kernel': jax.random.normal(ks[4], (NUM_EXPERTS, MLP, EMB), dtype=jnp.float32) / np.sqrt(MLP)}
    _L0_ffn_all = _L0_ffn_setup()
    _L0_ffn_in = {k: v for k, v in _L0_ffn_all.items() if k in ('gate_kernel', 'w0_kernel', 'w1_kernel', 'wo_kernel')}
    del _L0_ffn_all
    return {'x': x, 'ctx_2048': ctx_2048, 'L0_ffn_gate_kernel': _L0_ffn_in['gate_kernel'], 'L0_ffn_w0_kernel': _L0_ffn_in['w0_kernel'], 'L0_ffn_w1_kernel': _L0_ffn_in['w1_kernel'], 'L0_ffn_wo_kernel': _L0_ffn_in['wo_kernel']}

def reference(x, ctx_2048, L0_ffn_gate_kernel, L0_ffn_w0_kernel, L0_ffn_w1_kernel, L0_ffn_wo_kernel):
    import jax
    import jax.numpy as jnp

    def _L0_xattn_ref(q, k, v):
        import jax, jax.numpy as jnp
        import numpy as np
        N_HEAD = 8
        b, d, m = q.shape
        c = v.shape[1]
        h = N_HEAD
        qh = q.reshape(b * h, d // h, m)
        kh = k.reshape(b * h, d // h, -1)
        vh = v.reshape(b * h, c // h, -1)
        scale = 1.0 / jnp.sqrt(jnp.asarray(d // h, dtype=q.dtype))
        qk = jnp.einsum('bdm,bdn->bmn', qh, kh) * scale
        sm = jax.nn.softmax(qk, axis=-1)
        ret = jnp.einsum('bmn,bcn->bcm', sm, vh)
        return ret.reshape(b, c, m)

    def _L0_ffn_ref(x, gate_kernel, w0_kernel, w1_kernel, wo_kernel):
        import jax, jax.numpy as jnp
        import numpy as np
        NUM_EXPERTS = 8
        TOP_K = 2
        EMB = 256
        MLP = 512
        B, S = (4, 128)
        gate_logits = jnp.einsum('bsd,de->bse', x, gate_kernel)
        top_k_weights, top_k_indices = jax.lax.top_k(gate_logits, TOP_K)
        top_k_weights = jax.nn.softmax(top_k_weights.astype(jnp.float32), axis=-1).astype(x.dtype)
        one_hot = jax.nn.one_hot(top_k_indices, NUM_EXPERTS, dtype=x.dtype)
        combine = jnp.einsum('bsk,bske->bse', top_k_weights, one_hot)
        h0 = jnp.einsum('bsd,edm->bsem', x, w0_kernel)
        h1 = jnp.einsum('bsd,edm->bsem', x, w1_kernel)
        inter = jax.nn.silu(h0) * h1
        out = jnp.einsum('bse,bsem,emd->bsd', combine, inter, wo_kernel)
        return out
    x = x + _L0_xattn_ref(_layernorm(x, axis=-1), ctx_2048, ctx_2048)
    x = x + _L0_ffn_ref(_layernorm(x, axis=-1), L0_ffn_gate_kernel, L0_ffn_w0_kernel, L0_ffn_w1_kernel, L0_ffn_wo_kernel)
    return x

_drawn_inputs = setup_inputs


def setup_inputs(seed=0):
    import zlib

    import numpy as np

    out = dict(_drawn_inputs(seed))
    spreads = {}
    factors = {}
    for name, (base, spread) in spreads.items():
        noise = np.random.default_rng([zlib.crc32(name.encode()), seed]).standard_normal(out[name].shape)
        drawn = base * np.exp(spread * noise) if base else spread * noise
        out[name] = jnp.asarray(drawn.astype(out[name].dtype))
    for name, factor in factors.items():
        out[name] = (out[name] * factor).astype(out[name].dtype)
    return out
```

```python
import concourse.bass as bass
from concourse import mybir
from contextlib import ExitStack


def xattn_ffn_kernel(nc, x, ctx_in, gate_w, w0, w1, wo, out):
    f32 = mybir.dt.float32
    f16 = mybir.dt.float16
    bf16 = mybir.dt.bfloat16
    i32 = mybir.dt.int32
    u32 = mybir.dt.uint32
    ALU = mybir.AluOpType
    ACT = mybir.ActivationFunctionType
    AX = mybir.AxisListType

    P = 128
    B, S, M = x.shape
    HD = 8
    T = B * S // P
    ST = T // 2
    G = P // HD
    PAIRS = G // 2
    EPS = 1e-5
    SCALE = float(HD) ** -0.5
    QPARTS, KPARTS = 2, 3
    HR = QPARTS * KPARTS * HD
    KR = 2 * HR
    MXP = 2
    MXR = 2 * MXP
    MXSCALE = 2.0 ** 14
    LEAD = 10
    PTN = 8
    UNROLL = 6
    LOOPS = (T - 4) // UNROLL

    E, _, F = w0.shape
    TOPK = 2
    KC, FC = M // P, F // P
    NT = B * S * TOPK // P + E - 1
    PAY = 3
    WSCALE = 2.0 ** 12
    W_LOADS = 2 + LOOPS * UNROLL

    order = []
    for p in range(PAIRS):
        if p == 3:
            order.append(("max", 0))
        if p == 7:
            order.append(("max", 1))
        if p == 5:
            order += [("vt", 0), ("vt", 1)]
        order += [("exp", 2 * p), ("exp", 2 * p + 1)]
    RPT = len(order)
    RING0 = 4
    pos = {k: n for n, k in enumerate(order)}

    ctx = ExitStack()
    with ctx:
        def sb(name, shape, dt=f32):
            return ctx.enter_context(nc.sbuf_tensor(name, shape, dt))

        def sem(name):
            return ctx.enter_context(nc.semaphore(name))

        def rows_of(a):
            return a.rearrange("(t c) (q h d) m -> t h d (c q) m", c=2, h=2, d=HD)

        xq_view, ck_view = rows_of(x), rows_of(ctx_in)
        x_rows = x.rearrange("(s u c) r m -> s (c r) u m", u=2, c=2)

        c_rows = ctx_in.rearrange("(t c) r m -> t (c r) m", c=2)
        q_stack = nc.dram_tensor("q_stack", [ST, 2, QPARTS, KPARTS, P // 2, 2, M], f16).ap()
        k_stack = nc.dram_tensor("k_stack", [ST, 2, KPARTS, P // 2, 2, M], bf16).ap()
        acc = nc.dram_tensor("acc", [ST, 2 * G, HD + 1, M], f32).ap()
        rden = nc.dram_tensor("rden", [ST, 2 * G, M], f32).ap()

        xacc = nc.dram_tensor("xacc", [B * S + P, M], f32).ap()
        xrow = nc.dram_tensor("xrow", [B * S + 1, M], f32).ap()
        xacc_rows = xacc[0:B * S].rearrange("(s u p) m -> s p u m", u=2, p=P)
        xrow_rows = xrow[1:B * S + 1].rearrange("(s u p) m -> s p u m", u=2, p=P)

        q_sb = sb("q_sb", [P, T, M])
        w0_sb = sb("w0_sb", [P, E * KC, F])
        w1_sb = sb("w1_sb", [P, E * KC, F])
        wo_sb = sb("wo_sb", [P, E * FC, M])
        c_sb = wo_sb[:, 0:T, :]
        gate_sb = sb("gate_sb", [P, KC, E])
        v_sb = sb("v_sb", [P, 2, M])
        ident = sb("ident", [P, P])
        identh = sb("identh", [P, P], f16)
        mhalf = sb("mhalf", [P, T])
        stats = sb("stats", [P, T, 6])
        mv = sb("mv", [P, T, 2])
        veps = sb("veps", [P, T])
        rstd = sb("rstd", [P, T])
        res = sb("res", [P, 2, M])
        normed = sb("normed", [P, 2, M])
        qpart = sb("qpart", [P, QPARTS, 2, M], f16)
        kpart = sb("kpart", [P, KPARTS, 2, M], bf16)
        Q = [sb(f"Q{i}", [KR + MXR, PAIRS, M], f16) for i in range(3)]
        K = [sb(f"K{i}", [KR + MXR, 2, PAIRS, M], bf16) for i in range(3)]
        mx = sb("mx", [P, 2, 2, 2, 4])
        mp = sb("mp", [P, 2, 2, 2, MXP, 4], f16)
        mrow = sb("mrow", [MXR * 4, 2, M], f16)
        vT = [sb(f"vT{i}", [P, 2, G, HD + 1]) for i in range(3)]
        pt = sb("pt", [P, PTN, 2, M])
        pvs = sb("pvs", [P, 4, 2, M])
        den = sb("den", [P, 2 * M // HD])
        rd = sb("rd", [P, 2 * M // HD])
        rb = sb("rb", [P, 2, M])
        num = sb("num", [P, 2, M])
        xn = sb("xn", [P, 2, M])
        zero = sb("zero", [P, M])
        mone = sb("mone", [P, T])
        tri = sb("tri", [P, P], f16)
        ones = sb("ones", [P, P], f16)
        iota_e = sb("iota_e", [P, E])
        iota_s = sb("iota_s", [P, P], f16)
        iota_t = sb("iota_t", [P, NT], f16)
        token1 = sb("token1", [P, T], f16)
        dump = sb("dump", [P, 1])
        gT = sb("gT", [P, 2 * KC, P])
        top = sb("top", [P, 2, E])
        topi = sb("topi", [P, 2, E], u32)
        chosen = sb("chosen", [P, TOPK, T])
        gap = sb("gap", [P, T])
        e2 = sb("e2", [P, T])
        norm = sb("norm", [P, T])
        wts = sb("wts", [P, TOPK, T])
        pay = sb("pay", [P, PAY, TOPK, T], f16)
        A = sb("A", [P, TOPK, T, E])
        scan = [sb(f"scan{i}", [P, T // 2 + T, E]) for i in range(2)]
        rowcount = sb("rowcount", [P, E], f16)
        tiles_i = sb("tiles_i", [P, E], i32)
        ends = [sb(f"ends{i}", [P, E // 2 + E]) for i in range(2)]
        base = sb("base", [P, E])
        slot = sb("slot", [P, TOPK, T])
        slot_i = sb("slot_i", [P, 2, TOPK, T], i32)
        slot_f = sb("slot_f", [P, 2, TOPK, T])
        past_end = sb("past_end", [P, NT, E])
        expert_f = sb("expert_f", [P, NT])
        expert_of = sb("expert_of", [P, NT], i32)
        tok = sb("tok", [P, NT])
        empty = sb("empty", [P, NT])
        row_of = sb("row_of", [P, NT])
        wlow = sb("wlow", [P, NT])
        wslot = sb("wslot", [P, NT])
        gidx = [sb(f"gidx{i}", [P, 1], u32) for i in range(2)]
        sidx = [sb(f"sidx{i}", [P, 1], u32) for i in range(2)]

        half = pt[:, 0:PTN // 2].rearrange("p n u m -> p (n u m)")
        onehot_s = half.bitcast(f16).rearrange("p (k t s) -> p k t s", k=TOPK, t=T)
        rest = q_sb.rearrange("p t m -> p (t m)").bitcast(f16)
        n_oh = TOPK * T * NT
        onehot_t = rest[:, 0:n_oh].rearrange("p (k t i) -> p k t i", k=TOPK, t=T)
        told = rest[:, n_oh:(1 + PAY) * n_oh].rearrange("p (c k t i) -> p c k t i", c=PAY, k=TOPK, t=T)
        inter = [pt[:, i].rearrange("p u m -> p (u m)") for i in range(2)]
        sil = [pt[:, 2 + i].rearrange("p u m -> p (u m)") for i in range(2)]
        interT = [pt[:, 4 + i].rearrange("p u m -> p (u m)") for i in range(2)]
        xT = [pt[:, 6, i] for i in range(2)]
        gx = [pt[:, 7, i] for i in range(2)]
        y_sb = [rb[:, i] for i in range(2)]

        max_ps = [ctx.enter_context(nc.psum_tensor(f"max_ps{i}", [P, 2, 2, M], f32)) for i in range(2)]
        ring_ps = [ctx.enter_context(nc.psum_tensor(f"ring_ps{i}", [P, 2, M], f32)) for i in range(2)]
        pv_ps = [ctx.enter_context(nc.psum_tensor(f"pv_ps{i}", [P, 2, M], f32)) for i in range(2)]

        q_in = [sem(f"q_in{i}") for i in range(2)]
        v_in = [sem(f"v_in{i}") for i in range(2)]
        c_in = [sem(f"c_in{i}") for i in range(2)]
        consts = sem("consts")
        dve_fill = sem("dve_fill")
        fills = sem("fills")
        ln = sem("ln")
        veps_done = sem("veps_done")
        rstd_done = sem("rstd_done")
        qn_done = sem("qn_done")
        pool_fill = sem("pool_fill")
        k_chain = sem("k_chain")
        q_chain = sem("q_chain")
        q_split = sem("q_split")
        k_split = sem("k_split")
        stack_out = sem("stack_out")
        qk_in = [sem(f"qk_in{i}") for i in range(3)]
        max_full = sem("max_full")
        max_read = sem("max_read")
        mp_chain = sem("mp_chain")
        mp_done = sem("mp_done")
        ring_full = sem("ring_full")
        ring_read = sem("ring_read")
        mrow_in = [sem(f"mrow_in{i}") for i in range(2)]
        pv_full = sem("pv_full")
        pv_read = sem("pv_read")
        acc_out = sem("acc_out")
        den_in = sem("den_in")
        rd_done = sem("rd_done")
        rd_out = sem("rd_out")
        num_in = sem("num_in")
        prod_done = sem("prod_done")
        x2_done = sem("x2_done")
        x2_out = sem("x2_out")
        w_in = sem("w_in")
        sp_waited, pool_waited, dve_waited, pe_waited = (sem(n + "_waited") for n in ("sp", "pool", "dve", "pe"))
        zero_out = sem("zero_out")
        ln2 = sem("ln2")
        ln2_done = sem("ln2_done")
        row_out = sem("row_out")
        turned = sem("turned")
        gT_done = sem("gT_done")
        logits_full = sem("logits_full")
        top_chain = sem("top_chain")
        top_done = sem("top_done")
        gap_done = sem("gap_done")
        tables = sem("tables")
        norm_in = sem("norm_in")
        norm_done = sem("norm_done")
        e2_done = sem("e2_done")
        count_done = sem("count_done")
        ranks_full = sem("ranks_full")
        chain = sem("chain")
        told_done = sem("told_done")
        slots_full = sem("slots_full")
        slots_done = sem("slots_done")
        gidx_done = sem("gidx_done")
        gx_in = [sem(f"gx_in{i}") for i in range(2)]
        x_turned = sem("x_turned")
        xT_done = sem("xT_done")
        h0_full = sem("h0_full")
        h1_full = sem("h1_full")
        sil_done = sem("sil_done")
        inter_done = sem("inter_done")
        inter_turned = sem("inter_turned")
        interT_done = sem("interT_done")
        y_full = sem("y_full")
        y_done = sem("y_done")
        y_out = sem("y_out")
        copied = sem("copied")

        block = ctx.enter_context(nc.Block())

        class Step:

            def __init__(self, i, c):
                self.i, self.c = i, c
                self.t = i * UNROLL + c
                self.s = i * (UNROLL // 2) + c // 2
                self.half1 = self.s + 1
                self.third = i * (UNROLL // 3) + c // 3
                self.par, self.k = c % 2, c % 3
                self.peeled = isinstance(i, int)

            def at(self, d):
                return Step(self.i, self.c + d)

            def past(self, n):
                return not self.peeled or self.c >= n

            def before(self, n):
                return not self.peeled or self.c < n

        def run_steps(engine, step):
            step(Step(0, 0))
            with engine.Fori(0, LOOPS) as i:
                for c in range(1, UNROLL + 1):
                    step(Step(i, c))
            for c in range(UNROLL * LOOPS + 1, T):
                step(Step(0, c))

        def place(st, key):
            return key[1] if st.peeled and st.c == T - 1 else pos[key]

        def ring(st, key):
            return st.t * RPT + (RING0 + place(st, key))

        def bank(st, key):
            return ring_ps[place(st, key) % 2]

        def cols(a, t, n=1):
            return a[:, bass.ds(t, n), :]

        def flat(a):
            return a.rearrange("p u m -> p (u m)")

        class Slots:

            def __init__(self, i, c):
                self.i, self.c, self.t, self.par = i, c, 2 * i + c, c % 2
                self.upto = i + c // 2 + 1
                self.peeled = isinstance(i, int)

            def at(self, d):
                return Slots(self.i, self.c + d)

            def has(self, d):
                return not self.peeled or 0 <= self.t + d < NT

        def first_of(s):
            return isinstance(s, int)

        def all_pairs(engine, step):
            step(0)
            with engine.Fori(1, ST) as s:
                step(s)

        def run_slots(engine, step):
            for c in range(3):
                step(Slots(0, c))
            with engine.Fori(0, (NT - 5) // 2) as i:
                for c in (3, 4):
                    step(Slots(i, c))
            for c in range(NT - 2, NT + 1):
                step(Slots(0, c))

        @block.sync
        def _(sp):
            def load_heads(dst, view, done):
                for t in range(2):
                    for h in range(2):
                        sp.dma_start(dst[64 * h:64 * h + 64, t, :], view[t, h]).then_inc(done[0], 16)

            def load_rest(dst, view, done):
                for h in range(2):
                    for d in range(HD):
                        r = 64 * h + HD * d
                        sp.dma_start(dst[r:r + PAIRS, 2:T, :],
                                     view[2:T, h, d].rearrange("t p m -> p t m")).then_inc(done[1], 16)

            def store_stack(s):
                sp.wait_ge(k_split, s + 1)
                for h in range(2):
                    half = slice(64 * h, 64 * h + 64)
                    sp.dma_start(k_stack[bass.ds(s, 1), h].rearrange("o k p u m -> p (o k) (u m)"),
                                 kpart[half].rearrange("p k u m -> p k (u m)")).then_inc(stack_out, 16)
                sp.wait_ge(q_split, s + 1)
                for h in range(2):
                    half = slice(64 * h, 64 * h + 64)
                    for a in range(QPARTS):
                        sp.dma_start(q_stack[bass.ds(s, 1), h, a].rearrange("o k p u m -> p (o k) (u m)"),
                                     qpart[half, a:a + 1].rearrange("p k u m -> p k (u m)")
                                     .broadcast_to([64, KPARTS, 2 * M])).then_inc(stack_out, 16)

            def load_qk(st):
                sp.wait_ge(stack_out, (st.s + 1) * 96)
                q = q_stack[bass.ds(st.s, 1)].rearrange("o h a b (d p) u m -> (o h a b d) p u m", d=HD)
                sp.dma_start(Q[st.k][0:KR, :, :], q[:, :, st.par, :]).then_inc(qk_in[st.k], 16)
                for h in range(2):
                    k = k_stack[bass.ds(st.s, 1), h].rearrange("o b (d p) u m -> o (b d) p u m", d=HD)
                    for a in range(QPARTS):
                        r = HR * h + HR // 2 * a
                        sp.dma_start(K[st.k][r:r + HR // 2, h, :, :],
                                     k[0, :, :, st.par, :]).then_inc(qk_in[st.k], 16)

            def load_max(st, i, at):
                sp.wait_ge(ring_read, at + 1)
                sp.dma_start(Q[st.k][KR:KR + MXR, 4 * i:4 * i + 4, :], mrow[:, i, :]).then_inc(mrow_in[i], 16)

            def load_v(st):
                sp.dma_start(v_sb[:, st.par, :], c_rows[bass.ds(st.t, 1)].rearrange("o p m -> (o p) m")).then_inc(
                    v_in[st.par], 16)

            def store_acc(s):
                sp.wait_ge(pv_read, (s + 1) * 4)
                for j in range(4):
                    sp.dma_start(acc[bass.ds(s, 1)].rearrange("o (b j) r m -> j r (o b) m", j=4)[j],
                                 pvs[32 * j:32 * j + HD + 1].rearrange("p b f m -> p (b f) m")).then_inc(acc_out, 16)

            def load_den(s):
                sp.wait_ge(acc_out, (s + 1) * 64)
                sp.dma_start(den[:, :], acc[bass.ds(s, 1), :, HD, :]
                             .rearrange("o g (c m) -> (o g) c m", c=4)).then_inc(den_in, 16)

            def load_num(s, first):
                if not first:
                    sp.wait_ge(x2_done, s)
                for u in range(2):
                    sp.dma_start(num[:, u, :], acc[bass.ds(s, 1), G * u:G * u + G, 0:HD, :]
                                 .rearrange("o g r m -> (o g) r m")).then_inc(num_in, 16)
                sp.dma_start(xn[:, :, :], x_rows[bass.ds(s, 1)].rearrange("o p u m -> (o p) u m")).then_inc(num_in, 16)

            def scale_hop(s):
                sp.wait_ge(rd_done, s + 1)
                sp.dma_start(rden[bass.ds(s, 1)].rearrange("o g (c m) -> (o g c) m", c=4),
                             rd[:, :]).then_inc(rd_out, 16)
                sp.wait_ge(rd_out, (s + 1) * 16)
                for u in range(2):
                    sp.dma_start(rb[:, u, :], rden[bass.ds(s, 1), G * u:G * u + G]
                                 .rearrange("o g m -> (o g) m")[:, None, :].broadcast_to([G, HD, M])).then_inc(num_in, 16)

            def load_w(dst, w, a, n):
                sp.dma_start(dst[:, bass.ds(a, n), :], w[:, bass.ds(a, n), :]).then_inc(w_in, 16)

            w0_view = w0.rearrange("e (k p) f -> p (e k) f", p=P)
            w1_view = w1.rearrange("e (k p) f -> p (e k) f", p=P)
            wo_view = wo.rearrange("e (k p) m -> p (e k) m", p=P)

            load_heads(q_sb, xq_view, q_in)
            load_heads(c_sb, ck_view, c_in)
            load_rest(q_sb, xq_view, q_in)
            store_stack(0)
            sp.wait_ge(fills, 1)
            load_qk(Step(0, 0))
            load_rest(c_sb, ck_view, c_in)
            load_qk(Step(0, 1))
            store_stack(1)
            load_v(Step(0, 0))
            load_v(Step(0, 1))
            load_max(Step(0, 0), 0, 0)
            load_max(Step(0, 0), 1, 1)

            def step(st):
                sp.wait_ge(ring_full, ring(st, ("exp", 0)))
                sp.sem_inc(sp_waited, 1)
                if st.before(T - 2):
                    load_qk(st.at(2))
                    load_v(st.at(2))
                if st.past(1) and st.par == 0:
                    store_acc(st.at(-2).s)
                if st.before(T - 1):
                    load_max(st.at(1), 0, ring(st, ("max", 0)))
                if st.past(1) and st.par == 0:
                    load_den(st.at(-2).s)
                    load_num(st.at(-2).s, not st.past(3))
                    scale_hop(st.at(-2).s)
                if st.par == 1 and st.past(1) and st.before(T - 4):
                    store_stack(st.at(3).s)
                if st.before(T - 1):
                    load_max(st.at(1), 1, ring(st, ("max", 1)))
                if not st.peeled:
                    c, n = st.c - 1, E * KC // 2
                    if c < 4:
                        load_w((w0_sb, w1_sb)[c // 2], (w0_view, w1_view)[c // 2],
                               st.i * n + c % 2 * (n // 2), n // 2)
                    else:
                        load_w(wo_sb, wo_view, E * FC // 2 + st.i * (E * FC // 4) + (c - 4) * (E * FC // 8), E * FC // 8)
                elif st.c == T - 2:
                    sp.wait_ge(k_split, ST)
                    load_w(wo_sb, wo_view, 0, E * FC // 2)

            sp.wait_ge(fills, 1)
            sp.dma_start(gate_sb[:, :, :], gate_w.rearrange("(k p) e -> p k e", p=P)).then_inc(w_in, 16)
            sp.dma_start(xrow[0:1, :], zero[0:1, :]).then_inc(zero_out, 16)
            sp.dma_start(xacc[B * S:B * S + P, :], zero[:, :]).then_inc(zero_out, 16)
            run_steps(sp, step)
            store_acc(ST - 1)
            load_den(ST - 1)
            load_num(ST - 1, False)
            scale_hop(ST - 1)
            with sp.Fori(0, ST) as s:
                sp.wait_ge(ln2_done, s + 1)
                sp.dma_start(xrow_rows[bass.ds(s, 1)].rearrange("o p u m -> (o p) u m"),
                             normed[:, :, :]).then_inc(row_out, 16)
            sp.wait_ge(y_out, NT * 16)
            sp.dma_start(out.rearrange("b r m -> (b r) m"), xacc[0:B * S, :]).then_inc(copied, 16)
            sp.wait_ge(copied, 16)

        @block.gpsimd
        def _(g):
            g.memset(mhalf[:, :], -0.5).then_inc(pool_fill, 1)
            g.memset(ident[:, :], 0.0).then_inc(pool_fill, 1)
            g.memset(identh[:, :], 0.0).then_inc(pool_fill, 1)
            g.wait_ge(pool_fill, 3)
            for m in (ident, identh):
                g.affine_select(out=m[:, :], in_=m[:, :], compare_op=ALU.not_equal, fill=1.0,
                                base=0, pattern=[[-1, P]], channel_multiplier=1).then_inc(consts, 1)
            g.memset(mone[:, :], -1.0).then_inc(tables, 1)
            g.memset(ones[:, :], 1.0).then_inc(tables, 1)
            g.memset(tri[:, :], 1.0).then_inc(pool_fill, 1)
            g.wait_ge(pool_fill, 4)
            g.affine_select(out=tri[:, :], in_=tri[:, :], compare_op=ALU.is_gt, fill=0.0,
                            base=0, pattern=[[1, P]], channel_multiplier=-1).then_inc(tables, 1)
            for dst, pattern, first, step in ((iota_e, [[1, E]], 0, 0), (iota_s, [[1, P]], 0, 0), (iota_t, [[1, NT]], 0, 0),
                                              (token1, [[P, T]], 1, 1), (dump, [[0, 1]], B * S + 1, 1)):
                g.iota(dst[:, :], pattern, base=first, channel_multiplier=step,
                       allow_small_or_imprecise_dtypes=True).then_inc(tables, 1)

            def split_k(s):
                k = cols(c_sb, s * 2, 2)
                g.tensor_copy(kpart[:, 0], k).then_inc(k_chain, 1)
                g.wait_ge(k_chain, s * 3 + 1)
                g.sem_inc(pool_waited, 1)
                g.tensor_tensor(res[:, :, :], k, kpart[:, 0], ALU.subtract).then_inc(k_chain, 1)
                g.wait_ge(k_chain, s * 3 + 2)
                g.sem_inc(pool_waited, 1)
                g.tensor_copy(kpart[:, 1], res[:, :, :]).then_inc(k_chain, 1)
                g.wait_ge(k_chain, s * 3 + 3)
                g.sem_inc(pool_waited, 1)
                g.tensor_tensor(kpart[:, 2], res[:, :, :], kpart[:, 1], ALU.subtract).then_inc(k_split, 1)

            def split_q(s):
                q = cols(q_sb, s * 2, 2)
                g.tensor_copy(qpart[:, 0], q).then_inc(q_chain, 1)
                g.wait_ge(q_chain, s + 1)
                g.sem_inc(pool_waited, 1)
                g.tensor_tensor(qpart[:, 1], q, qpart[:, 0], ALU.subtract).then_inc(q_split, 1)

            def residual(s):
                g.wait_ge(num_in, (s + 1) * 80)
                g.tensor_tensor(num[:, :, :], num[:, :, :], rb[:, :, :], ALU.mult).then_inc(prod_done, 1)
                g.wait_ge(prod_done, s + 1)
                g.tensor_tensor(cols(q_sb, s * 2, 2), num[:, :, :], xn[:, :, :], ALU.add).then_inc(x2_done, 1)
                g.wait_ge(x2_done, s + 1)
                g.dma_start(xacc_rows[bass.ds(s, 1)].rearrange("o p u m -> (o p) u m"),
                            cols(q_sb, s * 2, 2)).then_inc(x2_out, 16)

            def prepare(s):
                g.wait_ge(stack_out, s * 96)
                split_k(s)
                split_q(s)

            def rsqrt(a, b, n):
                g.wait_ge(veps_done, n)
                g.tensor_tensor(rstd[:, a:b], veps[:, a:b], mhalf[:, a:b], ALU.pow).then_inc(rstd_done, 1)

            rsqrt(0, 2, 1)
            g.wait_ge(c_in[0], 64)
            split_k(0)
            rsqrt(2, T, 2)
            g.wait_ge(c_in[1], 256)
            g.wait_ge(qn_done, 2)
            for s in range(1, 4):
                prepare(s)
            residual(0)
            prepare(4)
            with g.Fori(5, ST) as s:
                residual(s - 4)
                prepare(s)
            with g.Fori(ST - 4, ST) as s:
                residual(s)
            with g.Fori(0, ST) as s:
                g.wait_ge(veps_done, s + 3)
                g.tensor_tensor(rstd[:, 0:2], veps[:, 0:2], mhalf[:, 0:2], ALU.pow).then_inc(rstd_done, 1)

            g.wait_ge(norm_in, 1)
            g.tensor_tensor(norm[:, :], norm[:, :], mone[:, :], ALU.pow).then_inc(norm_done, 1)

            def gather(sl):
                g.wait_ge(gidx_done, sl.t + 1)
                if sl.has(-2):
                    g.wait_ge(x_turned, sl.t - 1)
                g.sem_inc(pool_waited, 1)
                g.indirect_dma_start(gx[sl.par], None, xrow, bass.IndirectOffsetOnAxis(ap=gidx[sl.par][:, 0:1], axis=0)
                                     ).then_inc(gx_in[sl.par], 16)

            def scatter(sl):
                g.wait_ge(y_done, sl.t + 1)
                g.wait_ge(y_out, sl.t * 16)
                g.sem_inc(pool_waited, 1)
                g.indirect_dma_start(xacc, bass.IndirectOffsetOnAxis(ap=sidx[sl.par][:, 0:1], axis=0), y_sb[sl.par],
                                     None, compute_op=ALU.add).then_inc(y_out, 16)

            g.wait_ge(row_out, ST * 16)
            g.wait_ge(zero_out, 32)
            g.wait_ge(x2_out, ST * 16)
            gather(Slots(0, 0))
            gather(Slots(0, 1))

            def experts(sl):
                if sl.has(2):
                    gather(sl.at(2))
                if sl.has(-1):
                    scatter(sl.at(-1))

            run_slots(g, experts)

        @block.scalar
        def _(a):
            def evac_max(i, n, first):
                a.wait_ge(ring_full, n + 1)
                a.activation(mrow[:, i, :], ring_ps[i][0:MXR * 4, 0, 0:M // 2].bitcast(f16),
                             ACT.Copy).then_inc(ring_read, 1)

            def evac_v(k, j, par, n):
                a.wait_ge(ring_full, n + 1)
                a.activation(vT[k][:, j, :, 0:HD], ring_ps[par][:, 0, 0:P].rearrange("p (g d) -> p g d", d=HD),
                             ACT.Copy).then_inc(ring_read, 1)

            def exp(st, e):
                a.wait_ge(ring_full, ring(st, ("exp", e)) + 1)
                if e % 4 == 0 and (st.past(1) or e >= PTN):
                    a.wait_ge(pv_full, st.t * 4 + (e // 4 - 1))
                a.activation(pt[:, e % PTN, :, :], bank(st, ("exp", e))[:, :, :],
                             ACT.Exp, scale=SCALE).then_inc(ring_read, 1)

            def evac_pv(st, b):
                a.wait_ge(pv_full, st.t * 4 + (2 * b + 2))
                if st.past(2) and st.par == 0 and b == 0:
                    a.wait_ge(acc_out, st.s * 64)
                a.activation(pvs[:, 2 * st.par + b, :, :], pv_ps[b][:, :, :], ACT.Copy).then_inc(pv_read, 1)

            a.wait_ge(fills, 1)
            evac_max(0, 0, True)
            evac_max(1, 1, True)
            evac_v(0, 0, 0, 2)
            evac_v(0, 1, 1, 3)

            def step(st):
                for what, e in order:
                    if what == "exp":
                        exp(st, e)
                        if e == 3 and st.past(1):
                            evac_pv(st.at(-1), 1)
                        if e == 11:
                            evac_pv(st, 0)
                    elif st.before(T - 1):
                        n = ring(st, (what, e))
                        if what == "max":
                            a.wait_ge(mrow_in[e], (st.t + 1) * 16)
                            evac_max(e, n, False)
                        else:
                            evac_v((st.k + 1) % 3, e, pos[(what, e)] % 2, n)

            run_steps(a, step)
            evac_pv(Step(0, T - 1), 1)

            def evac_rows(s):
                a.wait_ge(turned, s + 1)
                if not first_of(s):
                    a.wait_ge(logits_full, s)
                a.activation(gT[:, :, :].rearrange("p k t -> p (k t)"), flat(max_ps[0][:, 0]), ACT.Copy).then_inc(gT_done, 1)

            all_pairs(a, evac_rows)
            a.wait_ge(gap_done, ST)
            a.activation(e2[:, :], gap[:, :], ACT.Exp).then_inc(e2_done, 1)

            def evac_x(sl):
                a.wait_ge(x_turned, sl.t + 1)
                if sl.has(-2):
                    a.wait_ge(h1_full, sl.t - 1)
                a.activation(xT[sl.par], ring_ps[1][:, 0, :], ACT.Copy).then_inc(xT_done, 1)

            def evac_inter(sl):
                a.wait_ge(inter_turned, sl.t + 1)
                if sl.has(-2):
                    a.wait_ge(y_full, sl.t - 1)
                a.activation(interT[sl.par], flat(ring_ps[0]), ACT.Copy).then_inc(interT_done, 1)

            evac_x(Slots(0, 0))

            def experts(sl):
                if sl.has(-1):
                    evac_inter(sl.at(-1))
                if sl.has(0):
                    a.wait_ge(h0_full, sl.t + 1)
                    if sl.has(-2):
                        a.wait_ge(inter_done, sl.t - 1)
                    a.activation(sil[sl.par], flat(max_ps[sl.par][:, 0]), ACT.Silu).then_inc(sil_done, 1)
                if sl.has(1):
                    evac_x(sl.at(1))

            run_slots(a, experts)

        @block.vector
        def _(v):
            for k in range(3):
                v.memset(K[k][:, :, :, :].rearrange("p h q m -> p (h q m)").bitcast(f32), 0.0).then_inc(dve_fill, 1)
            for k in range(3):
                v.memset(vT[k][:, :, :, HD:HD + 1], 1.0).then_inc(dve_fill, 1)
            for b in range(2):
                v.memset(pv_ps[b][:, :, :], 0.0).then_inc(dve_fill, 1)
            v.wait_ge(dve_fill, 3)
            for k in range(3):
                v.memset(K[k][KR:KR + MXR, 1, :, :], MXSCALE).then_inc(dve_fill, 1)
                v.memset(K[k][KR:KR + MXP, 0, :, :], MXSCALE).then_inc(dve_fill, 1)
            v.wait_ge(dve_fill, 14)
            for k in range(3):
                v.memset(K[k][KR:KR + MXP, 1, :, :], 0.0).then_inc(dve_fill, 1)
            v.wait_ge(dve_fill, 17)
            v.memset(zero[:, :], 0.0).then_inc(dve_fill, 1)
            v.wait_ge(dve_fill, 18)
            v.memset(mx[:, :, :, :, :], 0.0).then_inc(fills, 1)

            def ln1(a, b, done, before):
                n = b - a
                v.wait_ge(q_in[done], before)
                for t in range(a, b):
                    v.bn_stats(stats[:, t, :], q_sb[:, t, :]).then_inc(ln, 1)
                v.wait_ge(ln, a * 2 + n)
                for t in range(a, b):
                    v.bn_aggr(mv[:, t, :], stats[:, t, :]).then_inc(ln, 1)
                v.wait_ge(ln, 2 * b)
                v.tensor_scalar(veps[:, a:b], mv[:, a:b, 1], EPS, None, ALU.add).then_inc(veps_done, 1)

            def ln1_apply(a, b, done):
                v.wait_ge(rstd_done, done + 1)
                for t in range(a, b):
                    last = v.tensor_scalar(q_sb[:, t, :], q_sb[:, t, :], mv[:, t, 0:1], rstd[:, t:t + 1],
                                           ALU.subtract, ALU.mult)
                last.then_inc(qn_done, 1)

            ln1(0, 2, 0, 64)
            ln1_apply(0, 2, 0)
            v.wait_ge(qn_done, 1)
            v.tensor_copy(qpart[:, 0], q_sb[:, 0:2, :]).then_inc(q_chain, 1)
            v.wait_ge(q_chain, 1)
            v.tensor_tensor(qpart[:, 1], q_sb[:, 0:2, :], qpart[:, 0], ALU.subtract).then_inc(q_split, 1)
            ln1(2, T, 1, 256)
            ln1_apply(2, T, 1)

            def reduce(n, par, i, j):
                v.wait_ge(max_full, n + 1)
                v.tensor_reduce(mx[:, i, :, :, j], max_ps[par][:, :, :, :], axis=AX.X, op=ALU.max).then_inc(max_read, 1)

            def parts(u, i, n, at):
                v.wait_ge(max_read, n + 1)
                if at is not None:
                    v.wait_ge(ring_full, at + 1)
                v.tensor_scalar(mp[:, i, :, :, 0, :], mx[:, i, :, :, :], -1.0 / MXSCALE, None,
                                ALU.mult).then_inc(mp_chain, 1)
                v.wait_ge(mp_chain, u + 1)
                v.scalar_tensor_tensor(mp[:, i, :, :, 1, :], mx[:, i, :, :, :], -1.0 / MXSCALE, mp[:, i, :, :, 0, :],
                                       op0=ALU.mult, op1=ALU.subtract).then_inc(mp_done, 1)

            def recip(s, first):
                v.wait_ge(den_in, (s + 1) * 16)
                if not first:
                    v.wait_ge(rd_out, s * 16)
                v.reciprocal(rd[:, :], den[:, :]).then_inc(rd_done, 1)

            for n in range(LEAD):
                reduce(n, n % 2, (n // 4) % 2, n % 4)
                if n % 4 == 3:
                    parts(n // 4, (n // 4) % 2, n, None)

            def step(st):
                for p in range(PAIRS):
                    if st.before(T - 2) or (st.before(T - 1) and p + LEAD < 2 * PAIRS):
                        n = st.t * PAIRS + (p + LEAD)
                        reduce(n, p % 2, ((p + LEAD) // 4) % 2, (p + LEAD) % 4)
                        if p % 4 == 1:
                            i = p // 4
                            at = ring(st.at(-1), ("max", i)) if st.past(1) else i
                            parts(st.t * 2 + (2 + i), i, n, at)
                    if p == 5 and st.past(1) and st.par == 0:
                        recip(st.at(-2).s, not st.past(3))

            run_steps(v, step)
            recip(ST - 1, False)

            def normalise(s):
                v.wait_ge(x2_done, s + 1)
                for u in range(2):
                    v.bn_stats(stats[:, u, :], q_sb[:, bass.ds(s * 2 + u, 1), :].rearrange("p o m -> p (o m)")).then_inc(
                        ln2, 1)
                v.wait_ge(ln2, s * 4 + 2)
                v.sem_inc(dve_waited, 1)
                for u in range(2):
                    v.bn_aggr(mv[:, u, :], stats[:, u, :]).then_inc(ln2, 1)
                v.wait_ge(ln2, s * 4 + 4)
                v.tensor_scalar(veps[:, 0:2], mv[:, 0:2, 1], EPS, None, ALU.add).then_inc(veps_done, 1)
                v.wait_ge(rstd_done, s + 3)
                if not first_of(s):
                    v.wait_ge(row_out, s * 16)
                for u in range(2):
                    x2 = q_sb[:, bass.ds(s * 2 + u, 1), :].rearrange("p o m -> p (o m)")
                    last = v.tensor_scalar(normed[:, u, :], x2, mv[:, u, 0:1], rstd[:, u:u + 1], ALU.subtract, ALU.mult)
                last.then_inc(ln2_done, 1)
                v.wait_ge(logits_full, s + 1)
                v.sem_inc(dve_waited, 1)
                for u in range(2):
                    v.max(top[:, u, :], pv_ps[0][:, u, 0:E]).then_inc(top_chain, 1)
                v.wait_ge(top_chain, s * 4 + 2)
                v.tensor_tensor(gap[:, bass.ds(s * 2, 2)], top[:, :, 1], top[:, :, 0], ALU.subtract).then_inc(gap_done, 1)
                for u in range(2):
                    v.max_index(topi[:, u, :], top[:, u, :], pv_ps[0][:, u, 0:E]).then_inc(top_chain, 1)
                v.wait_ge(top_chain, s * 4 + 4)
                v.tensor_copy(chosen[:, :, bass.ds(s * 2, 2)],
                              topi[:, :, 0:TOPK].rearrange("p u k -> p k u")).then_inc(top_done, 1)

            all_pairs(v, normalise)

            links = [0]

            def then(op):
                links[0] += 1
                op.then_inc(chain, 1)
                v.wait_ge(chain, links[0])

            v.wait_ge(tables, 8)
            v.wait_ge(top_done, ST)
            for k in range(TOPK):
                then(v.tensor_tensor(A[:, k, :, :], chosen[:, k, :, None].broadcast_to([P, T, E]),
                                     iota_e[:, None, :].broadcast_to([P, T, E]), ALU.is_equal))
            lead = T // 2
            for i in range(2):
                then(v.memset(scan[i][:, 0:lead, :], 0.0))
            then(v.tensor_tensor(scan[0][:, lead:, :], A[:, 0], A[:, 1], ALU.add))
            src = 0
            shift = 1
            while shift < T:
                then(v.tensor_tensor(scan[1 - src][:, lead:, :], scan[src][:, lead:, :],
                                     scan[src][:, lead - shift:lead + T - shift, :], ALU.add))
                src = 1 - src
                shift *= 2
            v.tensor_copy(rowcount[:, :], scan[src][:, lead + T - 1, :]).then_inc(count_done, 1)
            v.wait_ge(e2_done, 1)
            v.tensor_scalar(norm[:, :], e2[:, :], 1.0, None, ALU.add).then_inc(norm_in, 1)
            v.wait_ge(ranks_full, 1)
            before, total = pv_ps[1][:, 0, 0:E], pv_ps[1][:, 0, E:2 * E]
            then(v.tensor_scalar(tiles_i[:, :], total, float(P - 1), None, ALU.add))
            then(v.tensor_scalar(tiles_i[:, :], tiles_i[:, :], P.bit_length() - 1, None, ALU.arith_shift_right))
            lead_e = E // 2
            for i in range(2):
                then(v.memset(ends[i][:, 0:lead_e], 0.0))
            then(v.tensor_copy(ends[0][:, lead_e:], tiles_i[:, :]))
            end = 0
            shift = 1
            while shift < E:
                then(v.tensor_tensor(ends[1 - end][:, lead_e:], ends[end][:, lead_e:],
                                     ends[end][:, lead_e - shift:lead_e + E - shift], ALU.add))
                end = 1 - end
                shift *= 2
            then(v.tensor_tensor(past_end[:, :, :], iota_t[:, :, None].broadcast_to([P, NT, E]),
                                 ends[end][:, None, lead_e:].broadcast_to([P, NT, E]), ALU.is_ge))
            then(v.tensor_reduce(expert_f[:, :], past_end[:, :, :], axis=AX.X, op=ALU.add))
            then(v.tensor_scalar(expert_of[:, :], expert_f[:, :], float(E - 1), None, ALU.min))
            then(v.tensor_scalar(base[:, :], ends[end][:, lead_e - 1:lead_e + E - 1], float(P), None, ALU.mult))
            then(v.tensor_tensor(base[:, :], base[:, :], before, ALU.add))
            then(v.tensor_tensor(scan[src][:, lead - 1:lead + T - 1, :], scan[src][:, lead - 1:lead + T - 1, :],
                                 base[:, None, :].broadcast_to([P, T, E]), ALU.add))
            for k in range(TOPK):
                then(v.tensor_tensor(A[:, k], A[:, k], scan[src][:, lead - 1:lead + T - 1, :], ALU.mult))
                then(v.tensor_reduce(slot[:, k, :], A[:, k], axis=AX.X, op=ALU.add))
            then(v.tensor_copy(slot_i[:, 0], slot[:, :, :]))
            then(v.tensor_scalar(slot_i[:, 1], slot_i[:, 0], P.bit_length() - 1, None, ALU.arith_shift_right))
            then(v.tensor_scalar(slot_i[:, 0], slot_i[:, 0], P - 1, None, ALU.bitwise_and))
            then(v.tensor_copy(slot_f[:, :], slot_i[:, :]))
            v.wait_ge(norm_done, 1)
            then(v.tensor_scalar(wts[:, 0, :], norm[:, :], WSCALE, None, ALU.mult))
            then(v.tensor_tensor(wts[:, 1, :], wts[:, 0, :], e2[:, :], ALU.mult))
            for k in range(TOPK):
                then(v.tensor_copy(pay[:, 0, k, :], token1[:, :]))
            then(v.tensor_copy(pay[:, 1], wts[:, :, :]))
            then(v.tensor_tensor(pay[:, 2], wts[:, :, :], pay[:, 1], ALU.subtract))
            v.wait_ge(x2_out, ST * 16)
            v.wait_ge(pv_full, T * 4)
            for k in range(TOPK):
                then(v.tensor_tensor(onehot_t[:, k], slot_f[:, 1, k, :, None].broadcast_to([P, T, NT]),
                                     iota_t[:, None, :].broadcast_to([P, T, NT]), ALU.is_equal))
            for c in range(PAY):
                for k in range(TOPK):
                    then(v.tensor_tensor(told[:, c, k], onehot_t[:, k],
                                         pay[:, c, k, :, None].broadcast_to([P, T, NT]), ALU.mult))
            for k in range(TOPK):
                for t in range(T):
                    v.tensor_scalar(onehot_s[:, k, t, :], iota_s[:, :], slot_f[:, 0, k, t:t + 1], None,
                                    ALU.is_equal).then_inc(told_done, 1)
            v.wait_ge(slots_full, 1)
            told_ps = pv_ps[0].rearrange("p u m -> p (u m)")[:, 0:PAY * NT].rearrange("p (c i) -> p c i", c=PAY)
            then(v.tensor_copy(tok[:, :], told_ps[:, 0, :]))
            then(v.tensor_copy(wlow[:, :], told_ps[:, 2, :]))
            then(v.scalar_tensor_tensor(wslot[:, :], told_ps[:, 1, :], 1.0, wlow[:, :], op0=ALU.mult, op1=ALU.add))
            then(v.tensor_scalar(wslot[:, :], wslot[:, :], 1.0 / WSCALE, None, ALU.mult))
            then(v.tensor_scalar(empty[:, :], tok[:, :], 0.0, dump[:, 0:1], ALU.is_equal, ALU.mult))
            then(v.scalar_tensor_tensor(row_of[:, :], tok[:, :], -1.0, empty[:, :], op0=ALU.add, op1=ALU.add))
            v.tensor_copy(tiles_i[0:1, 0:1], tiles_i[0:1, 0:1]).then_inc(slots_done, 1)

            def next_gather(sl):
                if sl.has(-2):
                    v.wait_ge(gx_in[sl.par], (sl.upto - 1) * 16)
                v.tensor_copy(gidx[sl.par][:, :], tok[:, bass.ds(sl.t, 1)]).then_inc(gidx_done, 1)

            next_gather(Slots(0, 0))
            next_gather(Slots(0, 1))

            def experts(sl):
                if sl.has(2):
                    next_gather(sl.at(2))
                if sl.has(0):
                    v.wait_ge(sil_done, sl.t + 1)
                    v.wait_ge(h1_full, sl.t + 1)
                    if sl.has(-2):
                        v.wait_ge(inter_turned, sl.t - 1)
                    v.tensor_tensor(inter[sl.par], sil[sl.par], flat(max_ps[sl.par][:, 1]), ALU.mult).then_inc(inter_done, 1)
                if sl.has(-1):
                    done = sl.at(-1)
                    v.wait_ge(y_full, done.t + 1)
                    if sl.has(-3):
                        v.wait_ge(y_out, (done.t - 1) * 16)
                    v.tensor_copy(sidx[done.par][:, :], row_of[:, bass.ds(done.t, 1)])
                    v.tensor_scalar(y_sb[done.par], pv_ps[done.par][:, 0, :], wslot[:, bass.ds(done.t, 1)], None,
                                    ALU.mult).then_inc(y_done, 1)

            run_slots(v, experts)

        @block.tensor
        def _(pe):
            def scores_max(n, st, p, par, first=False):
                if p == 0:
                    pe.wait_ge(qk_in[st.k], (st.third + 1) * 80)
                if not first:
                    pe.wait_ge(max_read, n - 1)
                for mt in range(2):
                    for h in range(2):
                        last = nc.tensor.matmul(max_ps[par][:, mt, h, :], lhsT=Q[st.k][0:KR, p, mt * P:(mt + 1) * P],
                                                rhs=K[st.k][0:KR, h, p, :], start=True, stop=True)
                last.then_inc(max_full, 1)

            def free_ring(n, first=False):
                if not first:
                    pe.wait_ge(ring_read, n - 1)

            def turn_max(u, i, n, first=False):
                free_ring(n, first)
                pe.wait_ge(mp_done, u + 1)
                for mt in range(2):
                    last = nc.tensor.transpose(ring_ps[i][0:MXR * 4, 0, 64 * mt:64 * mt + 64].bitcast(f16),
                                               mp[:, i, mt].rearrange("p h r j -> p (h r j)"), identh[:, :])
                last.then_inc(ring_full, 1)

            def turn_v(st, j, par, n):
                free_ring(n)
                if j == 0:
                    pe.wait_ge(v_in[st.par], st.half1 * 16)
                nc.tensor.transpose(ring_ps[par][:, 0, 0:P], v_sb[:, st.par, j * P:(j + 1) * P],
                                    ident[:, :]).then_inc(ring_full, 1)

            def scores_exp(st, e):
                p, h = e // 2, e % 2
                free_ring(ring(st, ("exp", e)))
                if e % 8 == 0:
                    pe.wait_ge(mrow_in[e // 8], (st.t + 1) * 16)
                for nt in range(2):
                    last = nc.tensor.matmul(bank(st, ("exp", e))[:, nt, :],
                                            lhsT=K[st.k][0:KR + MXR, h, p, nt * P:(nt + 1) * P],
                                            rhs=Q[st.k][:, p, :], start=True, stop=True)
                last.then_inc(ring_full, 1)

            def pv(st, q):
                pe.wait_ge(ring_read, ring(st, ("exp", 4 * q + 3)) + 1)
                if q % 2 == 0 and st.past(1):
                    pe.wait_ge(pv_read, st.t * 2 + (q // 2 - 1))
                for nt in range(2):
                    for j in range(4):
                        last = nc.tensor.matmul(pv_ps[q // 2][32 * j:32 * j + HD + 1, q % 2, :],
                                                lhsT=vT[st.k][:, nt, 4 * q + j, :], rhs=pt[:, (4 * q + j) % PTN, nt, :],
                                                start=(nt == 0), stop=(nt == 1))
                last.then_inc(pv_full, 1)

            pe.wait_ge(consts, 2)
            pe.wait_ge(fills, 1)
            for n in range(8):
                scores_max(n, Step(0, 0), n, n % 2, n < 2)
                if n == 6:
                    turn_max(0, 0, 0, True)
            scores_max(8, Step(0, 1), 0, 0)
            scores_max(9, Step(0, 1), 1, 1)
            turn_max(1, 1, 1, True)
            turn_v(Step(0, 0), 0, 0, 2)
            turn_v(Step(0, 0), 1, 1, 3)

            def step(st):
                for p in range(PAIRS):
                    if st.before(T - 2) or (st.before(T - 1) and p + LEAD < 2 * PAIRS):
                        scores_max(st.t * PAIRS + (p + LEAD), st.at((p + LEAD) // PAIRS), (p + LEAD) % PAIRS, p % 2)
                    if st.before(T - 1):
                        if p in (3, 7):
                            i = p // 4
                            turn_max(st.t * 2 + (2 + i), i, ring(st, ("max", i)))
                        if p == 5:
                            for j in range(2):
                                turn_v(st.at(1), j, place(st, ("vt", j)) % 2, ring(st, ("vt", j)))
                    for h in range(2):
                        scores_exp(st, 2 * p + h)
                    if p % 2 == 0 and p > 0:
                        pv(st, p // 2 - 1)
                    if p == 0 and st.past(1):
                        pv(st.at(-1), 3)

            run_steps(pe, step)
            pv(Step(0, T - 1), 3)

            pe.wait_ge(max_read, T * PAIRS)
            pe.wait_ge(pv_read, T * 2)
            pe.wait_ge(ring_read, RING0 + (T - 1) * RPT + G)
            pe.wait_ge(w_in, W_LOADS * 16)
            def logits(s):
                pe.wait_ge(ln2_done, s + 1)
                for u in range(2):
                    for k in range(KC):
                        last = nc.tensor.transpose(max_ps[0][:, 0, u, k * P:(k + 1) * P],
                                                   normed[:, u, k * P:(k + 1) * P], ident[:, :])
                last.then_inc(turned, 1)
                pe.wait_ge(gT_done, s + 1)
                if not first_of(s):
                    pe.wait_ge(top_done, s)
                for u in range(2):
                    for k in range(KC):
                        last = nc.tensor.matmul(pv_ps[0][:, u, 0:E], lhsT=gT[:, 2 * u + k, :], rhs=gate_sb[:, k, :],
                                                start=(k == 0), stop=(k == KC - 1))
                last.then_inc(logits_full, 1)

            all_pairs(pe, logits)
            pe.wait_ge(count_done, 1)
            pe.wait_ge(tables, 8)
            nc.tensor.matmul(pv_ps[1][:, 0, 0:E], lhsT=tri[:, :], rhs=rowcount[:, :], start=True, stop=True)
            nc.tensor.matmul(pv_ps[1][:, 0, E:2 * E], lhsT=ones[:, :], rhs=rowcount[:, :],
                             start=True, stop=True).then_inc(ranks_full, 1)
            pe.wait_ge(top_done, ST)
            for k in range(TOPK):
                for t in range(T):
                    n = k * T + t
                    pe.wait_ge(told_done, n + 1)
                    last = nc.tensor.matmul(pv_ps[0].rearrange("p u m -> p (u m)")[:, 0:PAY * NT]
                                            .rearrange("p (c i) -> p c i", c=PAY),
                                            lhsT=onehot_s[:, k, t, :], rhs=told[:, :, k, t, :],
                                            start=(n == 0), stop=(n == TOPK * T - 1))
            last.then_inc(slots_full, 1)

            def turn_x(sl):
                pe.wait_ge(gx_in[sl.par], sl.upto * 16)
                if sl.has(-1):
                    pe.wait_ge(xT_done, sl.t)
                for k in range(KC):
                    last = nc.tensor.transpose(ring_ps[1][:, 0, k * P:(k + 1) * P], gx[sl.par][:, k * P:(k + 1) * P],
                                               ident[:, :])
                last.then_inc(x_turned, 1)

            def turn_inter(sl):
                pe.wait_ge(inter_done, sl.t + 1)
                if sl.has(-1):
                    pe.wait_ge(interT_done, sl.t)
                for k in range(FC):
                    last = nc.tensor.transpose(flat(ring_ps[0])[:, k * P:(k + 1) * P], inter[sl.par][:, k * P:(k + 1) * P],
                                               ident[:, :])
                last.then_inc(inter_turned, 1)

            def expert(sl):
                return pe.value_load(expert_of[0:1, bass.ds(sl.t, 1)], min_val=0, max_val=E - 1)

            def weight(w, e, n, k):
                return w[:, bass.ds(e * n + k, 1), :].rearrange("p o m -> p (o m)")

            def hidden(sl):
                pe.wait_ge(xT_done, sl.t + 1)
                if sl.has(-2):
                    pe.wait_ge(inter_done, sl.t - 1)
                pe.sem_inc(pe_waited, 1)
                e = expert(sl)
                for w, bank_of, full in ((w0_sb, 0, h0_full), (w1_sb, 1, h1_full)):
                    for k in range(KC):
                        last = nc.tensor.matmul(flat(max_ps[sl.par][:, bank_of]), lhsT=xT[sl.par][:, k * P:(k + 1) * P],
                                                rhs=weight(w, e, KC, k), start=(k == 0), stop=(k == KC - 1))
                    last.then_inc(full, 1)

            def output(sl):
                pe.wait_ge(interT_done, sl.t + 1)
                if sl.has(-2):
                    pe.wait_ge(y_done, sl.t - 1)
                pe.sem_inc(pe_waited, 1)
                e = expert(sl)
                for k in range(FC):
                    last = nc.tensor.matmul(pv_ps[sl.par][:, 0, :], lhsT=interT[sl.par][:, k * P:(k + 1) * P],
                                            rhs=weight(wo_sb, e, FC, k), start=(k == 0), stop=(k == FC - 1))
                last.then_inc(y_full, 1)

            pe.wait_ge(slots_done, 1)
            turn_x(Slots(0, 0))

            def experts(sl):
                if sl.has(-1):
                    turn_inter(sl.at(-1))
                if sl.has(0):
                    hidden(sl)
                if sl.has(-1):
                    output(sl.at(-1))
                if sl.has(1):
                    turn_x(sl.at(1))

            run_slots(pe, experts)


def kernel(**inputs):
    import numpy as _np
    import concourse.bacc as _bacc
    from concourse import mybir as _mybir
    from concourse.bass_utils import run_bass_kernel_spmd as _run

    nc = _bacc.Bacc("TRN2", target_bir_lowering=False, num_devices=1)
    names = ["x", "ctx_2048", "L0_ffn_gate_kernel", "L0_ffn_w0_kernel", "L0_ffn_w1_kernel", "L0_ffn_wo_kernel"]
    arrays, args = {}, []
    for name in names:
        a = _np.ascontiguousarray(inputs[name])
        arrays[f"in_{name}"] = a
        args.append(nc.dram_tensor(f"in_{name}", a.shape, _mybir.dt.from_np(a.dtype), kind="ExternalInput").ap())
    shape = inputs["x"].shape
    args.append(nc.dram_tensor("out", shape, _mybir.dt.float32, kind="ExternalOutput").ap())
    xattn_ffn_kernel(nc, *args)
    r = _run(nc, [arrays], core_ids=[0])
    return r.results[0]["out"]
```

```python
import concourse.bass as bass
from concourse import mybir
from contextlib import ExitStack


def xattn_ffn_kernel(nc, x, ctx_in, gate_w, w0, w1, wo, out):
    f32 = mybir.dt.float32
    f16 = mybir.dt.float16
    bf16 = mybir.dt.bfloat16
    i32 = mybir.dt.int32
    u32 = mybir.dt.uint32
    ALU = mybir.AluOpType
    ACT = mybir.ActivationFunctionType
    AX = mybir.AxisListType

    P = 128
    B, S, M = x.shape
    HD = 8
    T = B * S // P
    ST = T // 2
    G = P // HD
    PAIRS = G // 2
    EPS = 1e-5
    SCALE = float(HD) ** -0.5
    QPARTS, KPARTS = 2, 3
    HR = QPARTS * KPARTS * HD
    KR = 2 * HR
    MXP = 2
    MXR = 2 * MXP
    MXSCALE = 2.0 ** 14
    LEAD = 10
    PTN = 8
    UNROLL = 6
    LOOPS = (T - 4) // UNROLL

    E, _, F = w0.shape
    TOPK = 2
    KC, FC = M // P, F // P
    NT = B * S * TOPK // P + E - 1
    PAY = 3
    WSCALE = 2.0 ** 12
    W_LOADS = 2 + LOOPS * UNROLL

    orders = ([], [])
    for even in (True, False):
        order = orders[not even]
        for p in range(PAIRS):
            if p == 3:
                order.append(("max", 0))
            if p == 7:
                order.append(("max", 1))
            if p == 5:
                order += [("vt", 0), ("vt", 1)]
            if even and p == 4:
                order.append(("rows", 0))
            if even and p == 6:
                order.append(("logits", 0))
            order += [("exp", 2 * p), ("exp", 2 * p + 1)]
    RPT = len(orders[1])
    RING0 = 4
    RING_END = RING0 + (T - 1) * RPT + T + G
    pos = [{k: n for n, k in enumerate(order)} for order in orders]
    LAG = 2

    ctx = ExitStack()
    with ctx:
        def sb(name, shape, dt=f32):
            return ctx.enter_context(nc.sbuf_tensor(name, shape, dt))

        def sem(name):
            return ctx.enter_context(nc.semaphore(name))

        def rows_of(a):
            return a.rearrange("(t c) (q h d) m -> t h d (c q) m", c=2, h=2, d=HD)

        xq_view, ck_view = rows_of(x), rows_of(ctx_in)
        x_rows = x.rearrange("(s u c) r m -> s (c r) u m", u=2, c=2)

        c_rows = ctx_in.rearrange("(t c) r m -> t (c r) m", c=2)
        q_stack = nc.dram_tensor("q_stack", [ST, 2, QPARTS, KPARTS, P // 2, 2, M], f16).ap()
        k_stack = nc.dram_tensor("k_stack", [ST, 2, KPARTS, P // 2, 2, M], bf16).ap()
        acc = nc.dram_tensor("acc", [ST, 2 * G, HD + 1, M], f32).ap()
        rden = nc.dram_tensor("rden", [ST, 2 * G, M], f32).ap()

        xacc = nc.dram_tensor("xacc", [B * S + P, M], f32).ap()
        ROW0 = LAG * 2 * P
        xrow = nc.dram_tensor("xrow", [ROW0 + B * S, M], f32).ap()
        xacc_rows = xacc[0:B * S].rearrange("(s u p) m -> s p u m", u=2, p=P)
        xrow_rows = xrow.rearrange("(s u p) m -> s p u m", u=2, p=P)

        q_sb = sb("q_sb", [P, T, M])
        w0_sb = sb("w0_sb", [P, E * KC, F])
        w1_sb = sb("w1_sb", [P, E * KC, F])
        wo_sb = sb("wo_sb", [P, E * FC, M])
        c_sb = wo_sb[:, 0:T, :]
        gate_sb = sb("gate_sb", [P, KC, E])
        v_sb = sb("v_sb", [P, 2, M])
        ident = sb("ident", [P, P])
        identh = sb("identh", [P, P], f16)
        mhalf = sb("mhalf", [P, T])
        stats = sb("stats", [P, T, 6])
        mv = sb("mv", [P, T, 2])
        veps = sb("veps", [P, T])
        rstd = sb("rstd", [P, T])
        res = sb("res", [P, 2, M])
        normed = sb("normed", [P, 2, M])
        qpart = sb("qpart", [P, QPARTS, 2, M], f16)
        kpart = sb("kpart", [P, KPARTS, 2, M], bf16)
        Q = [sb(f"Q{i}", [KR + MXR, PAIRS, M], f16) for i in range(3)]
        K = [sb(f"K{i}", [KR + MXR, 2, PAIRS, M], bf16) for i in range(3)]
        mx = sb("mx", [P, 2, 2, 2, 4])
        mp = sb("mp", [P, 2, 2, 2, MXP, 4], f16)
        mrow = sb("mrow", [MXR * 4, 2, M], f16)
        vT = [sb(f"vT{i}", [P, 2, G, HD + 1]) for i in range(3)]
        pt = sb("pt", [P, PTN, 2, M])
        pvs = sb("pvs", [P, 4, 2, M])
        den = sb("den", [P, 2 * M // HD])
        rd = sb("rd", [P, 2 * M // HD])
        rb = sb("rb", [P, 2, M])
        num = sb("num", [P, 2, M])
        xn = sb("xn", [P, 2, M])
        zero = sb("zero", [P, M])
        mone = sb("mone", [P, T])
        tri = sb("tri", [P, P], f16)
        ones = sb("ones", [P, P], f16)
        iota_e = sb("iota_e", [P, E])
        iota_s = sb("iota_s", [P, P], f16)
        iota_t = sb("iota_t", [P, NT], f16)
        token1 = sb("token1", [P, T], f16)
        dump = sb("dump", [P, 1])
        veps2 = sb("veps2", [P, 2])
        rstd2 = sb("rstd2", [P, 2])
        lgs = sb("lgs", [P, 2, E])
        top = sb("top", [P, 2, E])
        gT = q_sb[:, 0:2].rearrange("p u (k m) -> p (u k) m", m=P)
        x2 = q_sb[:, 2:4]
        topi = sb("topi", [P, 2, E], u32)
        chosen_all = sb("chosen_all", [P, TOPK, 2 * LAG + T])
        gap_all = sb("gap_all", [P, 2 * LAG + T])
        chosen, gap = chosen_all[:, :, 2 * LAG:], gap_all[:, 2 * LAG:]
        e2 = sb("e2", [P, T])
        norm = sb("norm", [P, T])
        wts = sb("wts", [P, TOPK, T])
        pay = sb("pay", [P, PAY, TOPK, T], f16)
        A = sb("A", [P, TOPK, T, E])
        scan = [sb(f"scan{i}", [P, T // 2 + T, E]) for i in range(2)]
        rowcount = sb("rowcount", [P, E], f16)
        tiles_i = sb("tiles_i", [P, E], i32)
        ends = [sb(f"ends{i}", [P, E // 2 + E]) for i in range(2)]
        base = sb("base", [P, E])
        slot = sb("slot", [P, TOPK, T])
        slot_i = sb("slot_i", [P, 2, TOPK, T], i32)
        slot_f = sb("slot_f", [P, 2, TOPK, T])
        past_end = sb("past_end", [P, NT, E])
        expert_f = sb("expert_f", [P, NT])
        expert_of = sb("expert_of", [P, NT], i32)
        tok = sb("tok", [P, NT])
        empty = sb("empty", [P, NT])
        row_of = sb("row_of", [P, NT])
        wlow = sb("wlow", [P, NT])
        wslot = sb("wslot", [P, NT])
        gidx = [sb(f"gidx{i}", [P, 1], u32) for i in range(2)]
        sidx = [sb(f"sidx{i}", [P, 1], u32) for i in range(2)]

        half = pt[:, 0:PTN // 2].rearrange("p n u m -> p (n u m)")
        onehot_s = half.bitcast(f16).rearrange("p (k t s) -> p k t s", k=TOPK, t=T)
        rest = q_sb.rearrange("p t m -> p (t m)").bitcast(f16)
        n_oh = TOPK * T * NT
        onehot_t = rest[:, 0:n_oh].rearrange("p (k t i) -> p k t i", k=TOPK, t=T)
        told = rest[:, n_oh:(1 + PAY) * n_oh].rearrange("p (c k t i) -> p c k t i", c=PAY, k=TOPK, t=T)
        inter = [pt[:, i].rearrange("p u m -> p (u m)") for i in range(2)]
        sil = [pt[:, 2 + i].rearrange("p u m -> p (u m)") for i in range(2)]
        interT = [pt[:, 4 + i].rearrange("p u m -> p (u m)") for i in range(2)]
        xT = [pt[:, 6, i] for i in range(2)]
        gx = [pt[:, 7, i] for i in range(2)]
        y_sb = [rb[:, i] for i in range(2)]

        max_ps = [ctx.enter_context(nc.psum_tensor(f"max_ps{i}", [P, 2, 2, M], f32)) for i in range(2)]
        ring_ps = [ctx.enter_context(nc.psum_tensor(f"ring_ps{i}", [P, 2, M], f32)) for i in range(2)]
        pv_ps = [ctx.enter_context(nc.psum_tensor(f"pv_ps{i}", [P, 2, M], f32)) for i in range(2)]

        q_in = [sem(f"q_in{i}") for i in range(2)]
        v_in = [sem(f"v_in{i}") for i in range(2)]
        c_in = [sem(f"c_in{i}") for i in range(2)]
        consts = sem("consts")
        dve_fill = sem("dve_fill")
        fills = sem("fills")
        ln = sem("ln")
        veps_done = sem("veps_done")
        rstd_done = sem("rstd_done")
        qn_done = sem("qn_done")
        pool_fill = sem("pool_fill")
        k_chain = sem("k_chain")
        q_chain = sem("q_chain")
        q_split = sem("q_split")
        k_split = sem("k_split")
        stack_out = sem("stack_out")
        qk_in = [sem(f"qk_in{i}") for i in range(3)]
        max_full = sem("max_full")
        max_read = sem("max_read")
        mp_chain = sem("mp_chain")
        mp_done = sem("mp_done")
        ring_full = sem("ring_full")
        ring_read = sem("ring_read")
        mrow_in = [sem(f"mrow_in{i}") for i in range(2)]
        pv_full = sem("pv_full")
        pv_read = sem("pv_read")
        acc_out = sem("acc_out")
        den_in = sem("den_in")
        rd_done = sem("rd_done")
        rd_out = sem("rd_out")
        num_in = sem("num_in")
        prod_done = sem("prod_done")
        x2_done = sem("x2_done")
        x2_out = sem("x2_out")
        w_in = sem("w_in")
        sp_waited, pool_waited, dve_waited, pe_waited = (sem(n + "_waited") for n in ("sp", "pool", "dve", "pe"))
        zero_out = sem("zero_out")
        ln2 = sem("ln2")
        ln2_done = sem("ln2_done")
        row_out = sem("row_out")
        veps2_done = sem("veps2_done")
        rstd2_done = sem("rstd2_done")
        top_chain = sem("top_chain")
        top_done = sem("top_done")
        gap_done = sem("gap_done")
        tables = sem("tables")
        norm_in = sem("norm_in")
        norm_done = sem("norm_done")
        e2_done = sem("e2_done")
        count_done = sem("count_done")
        ranks_full = sem("ranks_full")
        chain = sem("chain")
        told_done = sem("told_done")
        slots_full = sem("slots_full")
        slots_done = sem("slots_done")
        gidx_done = sem("gidx_done")
        gx_in = [sem(f"gx_in{i}") for i in range(2)]
        x_turned = sem("x_turned")
        xT_done = sem("xT_done")
        h0_full = sem("h0_full")
        h1_full = sem("h1_full")
        sil_done = sem("sil_done")
        inter_done = sem("inter_done")
        inter_turned = sem("inter_turned")
        interT_done = sem("interT_done")
        y_full = sem("y_full")
        y_done = sem("y_done")
        y_out = sem("y_out")
        copied = sem("copied")

        block = ctx.enter_context(nc.Block())

        class Step:

            def __init__(self, i, c):
                self.i, self.c = i, c
                self.t = i * UNROLL + c
                self.s = i * (UNROLL // 2) + c // 2
                self.half1 = self.s + 1
                self.evens = i * (UNROLL // 2) + (c + 1) // 2
                self.third = i * (UNROLL // 3) + c // 3
                self.par, self.k = c % 2, c % 3
                self.peeled = isinstance(i, int)

            def at(self, d):
                return Step(self.i, self.c + d)

            def past(self, n):
                return not self.peeled or self.c >= n

            def before(self, n):
                return not self.peeled or self.c < n

        def run_steps(engine, step):
            step(Step(0, 0))
            with engine.Fori(0, LOOPS) as i:
                for c in range(1, UNROLL + 1):
                    step(Step(i, c))
            for c in range(UNROLL * LOOPS + 1, T):
                step(Step(0, c))

        def place(st, key):
            return key[1] if st.peeled and st.c == T - 1 else pos[st.par][key]

        def ring(st, key):
            return st.t * RPT + st.evens * 2 + (RING0 + place(st, key))

        def bank(st, key):
            return ring_ps[place(st, key) % 2]

        def cols(a, t, n=1):
            return a[:, bass.ds(t, n), :]

        def flat(a):
            return a.rearrange("p u m -> p (u m)")

        class Slots:

            def __init__(self, i, c):
                self.i, self.c, self.t, self.par = i, c, 2 * i + c, c % 2
                self.upto = i + c // 2 + 1
                self.peeled = isinstance(i, int)

            def at(self, d):
                return Slots(self.i, self.c + d)

            def has(self, d):
                return not self.peeled or 0 <= self.t + d < NT

        def first_of(s):
            return isinstance(s, int)

        def run_slots(engine, step):
            for c in range(3):
                step(Slots(0, c))
            with engine.Fori(0, (NT - 5) // 2) as i:
                for c in (3, 4):
                    step(Slots(i, c))
            for c in range(NT - 2, NT + 1):
                step(Slots(0, c))

        @block.sync
        def _(sp):
            def load_heads(dst, view, done):
                for t in range(2):
                    for h in range(2):
                        sp.dma_start(dst[64 * h:64 * h + 64, t, :], view[t, h]).then_inc(done[0], 16)

            def load_rest(dst, view, done):
                for h in range(2):
                    for d in range(HD):
                        r = 64 * h + HD * d
                        sp.dma_start(dst[r:r + PAIRS, 2:T, :],
                                     view[2:T, h, d].rearrange("t p m -> p t m")).then_inc(done[1], 16)

            def store_stack(s):
                sp.wait_ge(k_split, s + 1)
                for h in range(2):
                    half = slice(64 * h, 64 * h + 64)
                    sp.dma_start(k_stack[bass.ds(s, 1), h].rearrange("o k p u m -> p (o k) (u m)"),
                                 kpart[half].rearrange("p k u m -> p k (u m)")).then_inc(stack_out, 16)
                sp.wait_ge(q_split, s + 1)
                for h in range(2):
                    half = slice(64 * h, 64 * h + 64)
                    for a in range(QPARTS):
                        sp.dma_start(q_stack[bass.ds(s, 1), h, a].rearrange("o k p u m -> p (o k) (u m)"),
                                     qpart[half, a:a + 1].rearrange("p k u m -> p k (u m)")
                                     .broadcast_to([64, KPARTS, 2 * M])).then_inc(stack_out, 16)

            def load_qk(st):
                sp.wait_ge(stack_out, (st.s + 1) * 96)
                q = q_stack[bass.ds(st.s, 1)].rearrange("o h a b (d p) u m -> (o h a b d) p u m", d=HD)
                sp.dma_start(Q[st.k][0:KR, :, :], q[:, :, st.par, :]).then_inc(qk_in[st.k], 16)
                for h in range(2):
                    k = k_stack[bass.ds(st.s, 1), h].rearrange("o b (d p) u m -> o (b d) p u m", d=HD)
                    for a in range(QPARTS):
                        r = HR * h + HR // 2 * a
                        sp.dma_start(K[st.k][r:r + HR // 2, h, :, :],
                                     k[0, :, :, st.par, :]).then_inc(qk_in[st.k], 16)

            def load_max(st, i, at):
                sp.wait_ge(ring_read, at + 1)
                sp.dma_start(Q[st.k][KR:KR + MXR, 4 * i:4 * i + 4, :], mrow[:, i, :]).then_inc(mrow_in[i], 16)

            def load_v(st):
                sp.dma_start(v_sb[:, st.par, :], c_rows[bass.ds(st.t, 1)].rearrange("o p m -> (o p) m")).then_inc(
                    v_in[st.par], 16)

            def store_rows(m):
                sp.wait_ge(ln2_done, m + 1)
                sp.dma_start(xrow_rows[bass.ds(m, 1)].rearrange("o p u m -> (o p) u m"),
                             normed[:, :, :]).then_inc(row_out, 16)

            def store_acc(s):
                sp.wait_ge(pv_read, (s + 1) * 4)
                for j in range(4):
                    sp.dma_start(acc[bass.ds(s, 1)].rearrange("o (b j) r m -> j r (o b) m", j=4)[j],
                                 pvs[32 * j:32 * j + HD + 1].rearrange("p b f m -> p (b f) m")).then_inc(acc_out, 16)

            def load_den(s):
                sp.wait_ge(acc_out, (s + 1) * 64)
                sp.dma_start(den[:, :], acc[bass.ds(s, 1), :, HD, :]
                             .rearrange("o g (c m) -> (o g) c m", c=4)).then_inc(den_in, 16)

            def load_num(s, first):
                if not first:
                    sp.wait_ge(x2_done, s + LAG)
                for u in range(2):
                    sp.dma_start(num[:, u, :], acc[bass.ds(s, 1), G * u:G * u + G, 0:HD, :]
                                 .rearrange("o g r m -> (o g) r m")).then_inc(num_in, 16)
                sp.dma_start(xn[:, :, :], x_rows[bass.ds(s, 1)].rearrange("o p u m -> (o p) u m")).then_inc(num_in, 16)

            def scale_hop(s):
                sp.wait_ge(rd_done, s + 1)
                sp.dma_start(rden[bass.ds(s, 1)].rearrange("o g (c m) -> (o g c) m", c=4),
                             rd[:, :]).then_inc(rd_out, 16)
                sp.wait_ge(rd_out, (s + 1) * 16)
                for u in range(2):
                    sp.dma_start(rb[:, u, :], rden[bass.ds(s, 1), G * u:G * u + G]
                                 .rearrange("o g m -> (o g) m")[:, None, :].broadcast_to([G, HD, M])).then_inc(num_in, 16)

            def load_w(dst, w, a, n):
                sp.dma_start(dst[:, bass.ds(a, n), :], w[:, bass.ds(a, n), :]).then_inc(w_in, 16)

            w0_view = w0.rearrange("e (k p) f -> p (e k) f", p=P)
            w1_view = w1.rearrange("e (k p) f -> p (e k) f", p=P)
            wo_view = wo.rearrange("e (k p) m -> p (e k) m", p=P)

            load_heads(q_sb, xq_view, q_in)
            load_heads(c_sb, ck_view, c_in)
            load_rest(q_sb, xq_view, q_in)
            store_stack(0)
            sp.wait_ge(fills, 1)
            load_qk(Step(0, 0))
            load_rest(c_sb, ck_view, c_in)
            load_qk(Step(0, 1))
            store_stack(1)
            load_v(Step(0, 0))
            load_v(Step(0, 1))
            load_max(Step(0, 0), 0, 0)
            load_max(Step(0, 0), 1, 1)

            def step(st):
                sp.wait_ge(ring_full, ring(st, ("exp", 0)))
                sp.sem_inc(sp_waited, 1)
                if st.before(T - 2):
                    load_qk(st.at(2))
                    load_v(st.at(2))
                if st.past(1) and st.par == 0:
                    store_acc(st.at(-2).s)
                if st.before(T - 1):
                    load_max(st.at(1), 0, ring(st, ("max", 0)))
                if st.past(1) and st.par == 0:
                    load_den(st.at(-2).s)
                    load_num(st.at(-2).s, not st.past(3))
                    scale_hop(st.at(-2).s)
                if st.par == 1 and st.past(1) and st.before(T - 4):
                    store_stack(st.at(3).s)
                if st.before(T - 1):
                    load_max(st.at(1), 1, ring(st, ("max", 1)))
                if st.par == 0:
                    store_rows(st.s)
                if not st.peeled:
                    c, n = st.c - 1, E * KC // 2
                    if c < 4:
                        load_w((w0_sb, w1_sb)[c // 2], (w0_view, w1_view)[c // 2],
                               st.i * n + c % 2 * (n // 2), n // 2)
                    else:
                        load_w(wo_sb, wo_view, E * FC // 2 + st.i * (E * FC // 4) + (c - 4) * (E * FC // 8), E * FC // 8)
                elif st.c == T - 2:
                    sp.wait_ge(k_split, ST)
                    load_w(wo_sb, wo_view, 0, E * FC // 2)

            sp.wait_ge(fills, 1)
            sp.dma_start(gate_sb[:, :, :], gate_w.rearrange("(k p) e -> p k e", p=P)).then_inc(w_in, 16)
            sp.dma_start(xacc[B * S:B * S + P, :], zero[:, :]).then_inc(zero_out, 16)
            run_steps(sp, step)
            store_acc(ST - 1)
            load_den(ST - 1)
            load_num(ST - 1, False)
            scale_hop(ST - 1)
            for m in range(ST, ST + LAG):
                store_rows(m)
            sp.wait_ge(row_out, (2 + ST) * 16)
            sp.dma_start(xrow[ROW0 - 1:ROW0, :], zero[0:1, :]).then_inc(zero_out, 16)
            sp.wait_ge(y_out, NT * 16)
            sp.dma_start(out.rearrange("b r m -> (b r) m"), xacc[0:B * S, :]).then_inc(copied, 16)
            sp.wait_ge(copied, 16)

        @block.gpsimd
        def _(g):
            g.memset(mhalf[:, :], -0.5).then_inc(pool_fill, 1)
            g.memset(ident[:, :], 0.0).then_inc(pool_fill, 1)
            g.memset(identh[:, :], 0.0).then_inc(pool_fill, 1)
            g.wait_ge(pool_fill, 3)
            for m in (ident, identh):
                g.affine_select(out=m[:, :], in_=m[:, :], compare_op=ALU.not_equal, fill=1.0,
                                base=0, pattern=[[-1, P]], channel_multiplier=1).then_inc(consts, 1)
            g.memset(mone[:, :], -1.0).then_inc(tables, 1)
            g.memset(ones[:, :], 1.0).then_inc(tables, 1)
            g.memset(tri[:, :], 1.0).then_inc(pool_fill, 1)
            g.wait_ge(pool_fill, 4)
            g.affine_select(out=tri[:, :], in_=tri[:, :], compare_op=ALU.is_gt, fill=0.0,
                            base=0, pattern=[[1, P]], channel_multiplier=-1).then_inc(tables, 1)
            for dst, pattern, first, step in ((iota_e, [[1, E]], 0, 0), (iota_s, [[1, P]], 0, 0), (iota_t, [[1, NT]], 0, 0),
                                              (token1, [[P, T]], 1, 1), (dump, [[0, 1]], B * S + 1, 1)):
                g.iota(dst[:, :], pattern, base=first, channel_multiplier=step,
                       allow_small_or_imprecise_dtypes=True).then_inc(tables, 1)

            def split_k(s):
                k = cols(c_sb, s * 2, 2)
                g.tensor_copy(kpart[:, 0], k).then_inc(k_chain, 1)
                g.wait_ge(k_chain, s * 3 + 1)
                g.sem_inc(pool_waited, 1)
                g.tensor_tensor(res[:, :, :], k, kpart[:, 0], ALU.subtract).then_inc(k_chain, 1)
                g.wait_ge(k_chain, s * 3 + 2)
                g.sem_inc(pool_waited, 1)
                g.tensor_copy(kpart[:, 1], res[:, :, :]).then_inc(k_chain, 1)
                g.wait_ge(k_chain, s * 3 + 3)
                g.sem_inc(pool_waited, 1)
                g.tensor_tensor(kpart[:, 2], res[:, :, :], kpart[:, 1], ALU.subtract).then_inc(k_split, 1)

            def split_q(s):
                q = cols(q_sb, s * 2, 2)
                g.tensor_copy(qpart[:, 0], q).then_inc(q_chain, 1)
                g.wait_ge(q_chain, s + 1)
                g.sem_inc(pool_waited, 1)
                g.tensor_tensor(qpart[:, 1], q, qpart[:, 0], ALU.subtract).then_inc(q_split, 1)

            def residual(s):
                g.wait_ge(num_in, (s + 1) * 80)
                g.tensor_tensor(num[:, :, :], num[:, :, :], rb[:, :, :], ALU.mult).then_inc(prod_done, 1)
                g.wait_ge(prod_done, s + 1)
                g.wait_ge(ln2_done, s + LAG)
                if not first_of(s):
                    g.wait_ge(x2_out, s * 16)
                g.sem_inc(pool_waited, 1)
                g.tensor_tensor(x2, num[:, :, :], xn[:, :, :], ALU.add).then_inc(x2_done, 1)
                g.wait_ge(x2_done, s + LAG + 1)
                g.dma_start(xacc_rows[bass.ds(s, 1)].rearrange("o p u m -> (o p) u m"), x2).then_inc(x2_out, 16)
                g.wait_ge(veps2_done, s + LAG + 1)
                g.sem_inc(pool_waited, 1)
                g.tensor_tensor(rstd2[:, :], veps2[:, :], mhalf[:, 0:2], ALU.pow).then_inc(rstd2_done, 1)

            def prepare(s):
                g.wait_ge(stack_out, s * 96)
                split_k(s)
                split_q(s)

            def rsqrt(a, b, n):
                g.wait_ge(veps_done, n)
                g.tensor_tensor(rstd[:, a:b], veps[:, a:b], mhalf[:, a:b], ALU.pow).then_inc(rstd_done, 1)

            rsqrt(0, 2, 1)
            g.wait_ge(c_in[0], 64)
            split_k(0)
            rsqrt(2, T, 2)
            g.wait_ge(c_in[1], 256)
            g.wait_ge(qn_done, 2)
            for s in range(1, 4):
                prepare(s)
            residual(0)
            prepare(4)
            with g.Fori(5, ST) as s:
                residual(s - 4)
                prepare(s)
            with g.Fori(ST - 4, ST) as s:
                residual(s)
            g.wait_ge(norm_in, 1)
            g.tensor_tensor(norm[:, :], norm[:, :], mone[:, :], ALU.pow).then_inc(norm_done, 1)

            def gather(sl):
                g.wait_ge(gidx_done, sl.t + 1)
                if sl.has(-2):
                    g.wait_ge(x_turned, sl.t - 1)
                g.sem_inc(pool_waited, 1)
                g.indirect_dma_start(gx[sl.par], None, xrow, bass.IndirectOffsetOnAxis(ap=gidx[sl.par][:, 0:1], axis=0)
                                     ).then_inc(gx_in[sl.par], 16)

            def scatter(sl):
                g.wait_ge(y_done, sl.t + 1)
                g.wait_ge(y_out, sl.t * 16)
                g.sem_inc(pool_waited, 1)
                g.indirect_dma_start(xacc, bass.IndirectOffsetOnAxis(ap=sidx[sl.par][:, 0:1], axis=0), y_sb[sl.par],
                                     None, compute_op=ALU.add).then_inc(y_out, 16)

            g.wait_ge(row_out, (1 + LAG + ST) * 16)
            g.wait_ge(zero_out, 32)
            g.wait_ge(x2_out, ST * 16)
            gather(Slots(0, 0))
            gather(Slots(0, 1))

            def experts(sl):
                if sl.has(2):
                    gather(sl.at(2))
                if sl.has(-1):
                    scatter(sl.at(-1))

            run_slots(g, experts)

        @block.scalar
        def _(a):
            def evac_max(i, n, first):
                a.wait_ge(ring_full, n + 1)
                a.activation(mrow[:, i, :], ring_ps[i][0:MXR * 4, 0, 0:M // 2].bitcast(f16),
                             ACT.Copy).then_inc(ring_read, 1)

            def evac_v(k, j, par, n):
                a.wait_ge(ring_full, n + 1)
                a.activation(vT[k][:, j, :, 0:HD], ring_ps[par][:, 0, 0:P].rearrange("p (g d) -> p g d", d=HD),
                             ACT.Copy).then_inc(ring_read, 1)

            def evac_rows(par, n):
                a.wait_ge(ring_full, n + 1)
                a.activation(gT.rearrange("p k t -> p (k t)"), flat(ring_ps[par]), ACT.Copy).then_inc(ring_read, 1)

            def evac_logits(par, n, m):
                a.wait_ge(ring_full, n + 1)
                a.wait_ge(top_done, m + 1)
                a.activation(lgs[:, :, :], ring_ps[par][:, :, 0:E], ACT.Copy).then_inc(ring_read, 1)

            def exp(st, e):
                a.wait_ge(ring_full, ring(st, ("exp", e)) + 1)
                if e % 4 == 0 and (st.past(1) or e >= PTN):
                    a.wait_ge(pv_full, st.t * 4 + (e // 4 - 1))
                a.activation(pt[:, e % PTN, :, :], bank(st, ("exp", e))[:, :, :],
                             ACT.Exp, scale=SCALE).then_inc(ring_read, 1)

            def evac_pv(st, b):
                a.wait_ge(pv_full, st.t * 4 + (2 * b + 2))
                if st.past(2) and st.par == 0 and b == 0:
                    a.wait_ge(acc_out, st.s * 64)
                a.activation(pvs[:, 2 * st.par + b, :, :], pv_ps[b][:, :, :], ACT.Copy).then_inc(pv_read, 1)

            a.wait_ge(fills, 1)
            evac_max(0, 0, True)
            evac_max(1, 1, True)
            evac_v(0, 0, 0, 2)
            evac_v(0, 1, 1, 3)

            def step(st):
                for what, e in orders[st.par]:
                    if what == "exp":
                        exp(st, e)
                        if e == 3 and st.past(1):
                            evac_pv(st.at(-1), 1)
                        if e == 11:
                            evac_pv(st, 0)
                    elif st.before(T - 1):
                        n = ring(st, (what, e))
                        if what == "max":
                            a.wait_ge(mrow_in[e], (st.t + 1) * 16)
                            evac_max(e, n, False)
                        elif what == "rows":
                            evac_rows(place(st, (what, e)) % 2, n)
                        elif what == "logits":
                            evac_logits(place(st, (what, e)) % 2, n, st.s)
                        else:
                            evac_v((st.k + 1) % 3, e, pos[st.par][(what, e)] % 2, n)

            run_steps(a, step)
            evac_pv(Step(0, T - 1), 1)

            for i in range(LAG):
                evac_rows(0, RING_END + 2 * i)
                evac_logits(1, RING_END + 2 * i + 1, ST + i)
            a.wait_ge(gap_done, LAG + ST)
            a.activation(e2[:, :], gap[:, :], ACT.Exp).then_inc(e2_done, 1)

            def evac_x(sl):
                a.wait_ge(x_turned, sl.t + 1)
                if sl.has(-2):
                    a.wait_ge(h1_full, sl.t - 1)
                a.activation(xT[sl.par], ring_ps[1][:, 0, :], ACT.Copy).then_inc(xT_done, 1)

            def evac_inter(sl):
                a.wait_ge(inter_turned, sl.t + 1)
                if sl.has(-2):
                    a.wait_ge(y_full, sl.t - 1)
                a.activation(interT[sl.par], flat(ring_ps[0]), ACT.Copy).then_inc(interT_done, 1)

            evac_x(Slots(0, 0))

            def experts(sl):
                if sl.has(-1):
                    evac_inter(sl.at(-1))
                if sl.has(0):
                    a.wait_ge(h0_full, sl.t + 1)
                    if sl.has(-2):
                        a.wait_ge(inter_done, sl.t - 1)
                    a.activation(sil[sl.par], flat(max_ps[sl.par][:, 0]), ACT.Silu).then_inc(sil_done, 1)
                if sl.has(1):
                    evac_x(sl.at(1))

            run_slots(a, experts)

        @block.vector
        def _(v):
            for k in range(3):
                v.memset(K[k][:, :, :, :].rearrange("p h q m -> p (h q m)").bitcast(f32), 0.0).then_inc(dve_fill, 1)
            for k in range(3):
                v.memset(vT[k][:, :, :, HD:HD + 1], 1.0).then_inc(dve_fill, 1)
            for b in range(2):
                v.memset(pv_ps[b][:, :, :], 0.0).then_inc(dve_fill, 1)
            v.wait_ge(dve_fill, 3)
            for k in range(3):
                v.memset(K[k][KR:KR + MXR, 1, :, :], MXSCALE).then_inc(dve_fill, 1)
                v.memset(K[k][KR:KR + MXP, 0, :, :], MXSCALE).then_inc(dve_fill, 1)
            v.wait_ge(dve_fill, 14)
            for k in range(3):
                v.memset(K[k][KR:KR + MXP, 1, :, :], 0.0).then_inc(dve_fill, 1)
            v.wait_ge(dve_fill, 17)
            v.memset(zero[:, :], 0.0).then_inc(dve_fill, 1)
            v.memset(rstd2[:, :], 1.0).then_inc(dve_fill, 1)
            v.wait_ge(dve_fill, 19)
            v.memset(mx[:, :, :, :, :], 0.0).then_inc(fills, 1)

            def ln1(a, b, done, before):
                n = b - a
                v.wait_ge(q_in[done], before)
                for t in range(a, b):
                    v.bn_stats(stats[:, t, :], q_sb[:, t, :]).then_inc(ln, 1)
                v.wait_ge(ln, a * 2 + n)
                for t in range(a, b):
                    v.bn_aggr(mv[:, t, :], stats[:, t, :]).then_inc(ln, 1)
                v.wait_ge(ln, 2 * b)
                v.tensor_scalar(veps[:, a:b], mv[:, a:b, 1], EPS, None, ALU.add).then_inc(veps_done, 1)

            def ln1_apply(a, b, done):
                v.wait_ge(rstd_done, done + 1)
                for t in range(a, b):
                    last = v.tensor_scalar(q_sb[:, t, :], q_sb[:, t, :], mv[:, t, 0:1], rstd[:, t:t + 1],
                                           ALU.subtract, ALU.mult)
                last.then_inc(qn_done, 1)

            ln1(0, 2, 0, 64)
            ln1_apply(0, 2, 0)
            v.wait_ge(qn_done, 1)
            v.tensor_copy(qpart[:, 0], q_sb[:, 0:2, :]).then_inc(q_chain, 1)
            v.wait_ge(q_chain, 1)
            v.tensor_tensor(qpart[:, 1], q_sb[:, 0:2, :], qpart[:, 0], ALU.subtract).then_inc(q_split, 1)
            ln1(2, T, 1, 256)
            ln1_apply(2, T, 1)

            def reduce(n, par, i, j):
                v.wait_ge(max_full, n + 1)
                v.tensor_reduce(mx[:, i, :, :, j], max_ps[par][:, :, :, :], axis=AX.X, op=ALU.max).then_inc(max_read, 1)

            def parts(u, i, n, at):
                v.wait_ge(max_read, n + 1)
                if at is not None:
                    v.wait_ge(ring_full, at + 1)
                v.tensor_scalar(mp[:, i, :, :, 0, :], mx[:, i, :, :, :], -1.0 / MXSCALE, None,
                                ALU.mult).then_inc(mp_chain, 1)
                v.wait_ge(mp_chain, u + 1)
                v.scalar_tensor_tensor(mp[:, i, :, :, 1, :], mx[:, i, :, :, :], -1.0 / MXSCALE, mp[:, i, :, :, 0, :],
                                       op0=ALU.mult, op1=ALU.subtract).then_inc(mp_done, 1)

            def rows_stats(m):
                v.wait_ge(x2_done, m + 1)
                for u in range(2):
                    v.bn_stats(stats[:, u, :], x2[:, u, :]).then_inc(ln2, 1)
                v.wait_ge(ln2, m * 4 + 2)
                v.sem_inc(dve_waited, 1)
                for u in range(2):
                    v.bn_aggr(mv[:, u, :], stats[:, u, :]).then_inc(ln2, 1)
                v.wait_ge(ln2, m * 4 + 4)
                v.tensor_scalar(veps2[:, :], mv[:, 0:2, 1], EPS, None, ALU.add).then_inc(veps2_done, 1)

            def rows_apply(m):
                v.wait_ge(rstd2_done, m + 1)
                v.wait_ge(row_out, (m + 1) * 16)
                for u in range(2):
                    last = v.tensor_scalar(normed[:, u, :], x2[:, u, :], mv[:, u, 0:1], rstd2[:, u:u + 1],
                                           ALU.subtract, ALU.mult)
                last.then_inc(ln2_done, 1)

            def choose(m, n):
                v.wait_ge(ring_read, n + 1)
                v.sem_inc(dve_waited, 1)
                for u in range(2):
                    v.max(top[:, u, :], lgs[:, u, :]).then_inc(top_chain, 1)
                v.wait_ge(top_chain, m * 4 + 2)
                v.tensor_tensor(gap_all[:, bass.ds(m * 2, 2)], top[:, :, 1], top[:, :, 0], ALU.subtract).then_inc(gap_done, 1)
                for u in range(2):
                    v.max_index(topi[:, u, :], top[:, u, :], lgs[:, u, :]).then_inc(top_chain, 1)
                v.wait_ge(top_chain, m * 4 + 4)
                v.tensor_copy(chosen_all[:, :, bass.ds(m * 2, 2)],
                              topi[:, :, 0:TOPK].rearrange("p u k -> p k u")).then_inc(top_done, 1)

            def recip(s, first):
                v.wait_ge(den_in, (s + 1) * 16)
                if not first:
                    v.wait_ge(rd_out, s * 16)
                v.reciprocal(rd[:, :], den[:, :]).then_inc(rd_done, 1)

            for n in range(LEAD):
                reduce(n, n % 2, (n // 4) % 2, n % 4)
                if n % 4 == 3:
                    parts(n // 4, (n // 4) % 2, n, None)

            def step(st):
                for p in range(PAIRS):
                    if st.before(T - 2) or (st.before(T - 1) and p + LEAD < 2 * PAIRS):
                        n = st.t * PAIRS + (p + LEAD)
                        reduce(n, p % 2, ((p + LEAD) // 4) % 2, (p + LEAD) % 4)
                        if p % 4 == 1:
                            i = p // 4
                            at = ring(st.at(-1), ("max", i)) if st.past(1) else i
                            parts(st.t * 2 + (2 + i), i, n, at)
                    if st.par == 0 and p == 1:
                        rows_stats(st.s)
                    if st.par == 0 and p == 3:
                        rows_apply(st.s)
                    if p == 0 and st.par == 1:
                        choose(st.at(-1).s, ring(st.at(-1), ("logits", 0)))
                    if p == 5 and st.past(1) and st.par == 0:
                        recip(st.at(-2).s, not st.past(3))

            v.sem_inc(x2_done, LAG)
            v.sem_inc(rstd2_done, LAG)
            v.sem_inc(row_out, 16)
            v.sem_inc(top_done, 1)
            v.wait_ge(qn_done, 2)
            run_steps(v, step)
            recip(ST - 1, False)

            for m in range(ST, ST + LAG):
                rows_stats(m)
                rows_apply(m)
                choose(m, RING_END + 2 * (m - ST) + 1)

            links = [0]

            def then(op):
                links[0] += 1
                op.then_inc(chain, 1)
                v.wait_ge(chain, links[0])

            v.wait_ge(tables, 8)
            v.wait_ge(top_done, 1 + LAG + ST)
            for k in range(TOPK):
                then(v.tensor_tensor(A[:, k, :, :], chosen[:, k, :, None].broadcast_to([P, T, E]),
                                     iota_e[:, None, :].broadcast_to([P, T, E]), ALU.is_equal))
            lead = T // 2
            for i in range(2):
                then(v.memset(scan[i][:, 0:lead, :], 0.0))
            then(v.tensor_tensor(scan[0][:, lead:, :], A[:, 0], A[:, 1], ALU.add))
            src = 0
            shift = 1
            while shift < T:
                then(v.tensor_tensor(scan[1 - src][:, lead:, :], scan[src][:, lead:, :],
                                     scan[src][:, lead - shift:lead + T - shift, :], ALU.add))
                src = 1 - src
                shift *= 2
            v.tensor_copy(rowcount[:, :], scan[src][:, lead + T - 1, :]).then_inc(count_done, 1)
            v.wait_ge(e2_done, 1)
            v.tensor_scalar(norm[:, :], e2[:, :], 1.0, None, ALU.add).then_inc(norm_in, 1)
            v.wait_ge(ranks_full, 1)
            before, total = pv_ps[1][:, 0, 0:E], pv_ps[1][:, 0, E:2 * E]
            then(v.tensor_scalar(tiles_i[:, :], total, float(P - 1), None, ALU.add))
            then(v.tensor_scalar(tiles_i[:, :], tiles_i[:, :], P.bit_length() - 1, None, ALU.arith_shift_right))
            lead_e = E // 2
            for i in range(2):
                then(v.memset(ends[i][:, 0:lead_e], 0.0))
            then(v.tensor_copy(ends[0][:, lead_e:], tiles_i[:, :]))
            end = 0
            shift = 1
            while shift < E:
                then(v.tensor_tensor(ends[1 - end][:, lead_e:], ends[end][:, lead_e:],
                                     ends[end][:, lead_e - shift:lead_e + E - shift], ALU.add))
                end = 1 - end
                shift *= 2
            then(v.tensor_tensor(past_end[:, :, :], iota_t[:, :, None].broadcast_to([P, NT, E]),
                                 ends[end][:, None, lead_e:].broadcast_to([P, NT, E]), ALU.is_ge))
            then(v.tensor_reduce(expert_f[:, :], past_end[:, :, :], axis=AX.X, op=ALU.add))
            then(v.tensor_scalar(expert_of[:, :], expert_f[:, :], float(E - 1), None, ALU.min))
            then(v.tensor_scalar(base[:, :], ends[end][:, lead_e - 1:lead_e + E - 1], float(P), None, ALU.mult))
            then(v.tensor_tensor(base[:, :], base[:, :], before, ALU.add))
            then(v.tensor_tensor(scan[src][:, lead - 1:lead + T - 1, :], scan[src][:, lead - 1:lead + T - 1, :],
                                 base[:, None, :].broadcast_to([P, T, E]), ALU.add))
            for k in range(TOPK):
                then(v.tensor_tensor(A[:, k], A[:, k], scan[src][:, lead - 1:lead + T - 1, :], ALU.mult))
                then(v.tensor_reduce(slot[:, k, :], A[:, k], axis=AX.X, op=ALU.add))
            then(v.tensor_copy(slot_i[:, 0], slot[:, :, :]))
            then(v.tensor_scalar(slot_i[:, 1], slot_i[:, 0], P.bit_length() - 1, None, ALU.arith_shift_right))
            then(v.tensor_scalar(slot_i[:, 0], slot_i[:, 0], P - 1, None, ALU.bitwise_and))
            then(v.tensor_copy(slot_f[:, :], slot_i[:, :]))
            v.wait_ge(norm_done, 1)
            then(v.tensor_scalar(wts[:, 0, :], norm[:, :], WSCALE, None, ALU.mult))
            then(v.tensor_tensor(wts[:, 1, :], wts[:, 0, :], e2[:, :], ALU.mult))
            for k in range(TOPK):
                then(v.tensor_copy(pay[:, 0, k, :], token1[:, :]))
            then(v.tensor_copy(pay[:, 1], wts[:, :, :]))
            then(v.tensor_tensor(pay[:, 2], wts[:, :, :], pay[:, 1], ALU.subtract))
            v.wait_ge(row_out, (1 + LAG + ST) * 16)
            v.wait_ge(x2_out, ST * 16)
            v.wait_ge(pv_full, T * 4)
            for k in range(TOPK):
                then(v.tensor_tensor(onehot_t[:, k], slot_f[:, 1, k, :, None].broadcast_to([P, T, NT]),
                                     iota_t[:, None, :].broadcast_to([P, T, NT]), ALU.is_equal))
            for c in range(PAY):
                for k in range(TOPK):
                    then(v.tensor_tensor(told[:, c, k], onehot_t[:, k],
                                         pay[:, c, k, :, None].broadcast_to([P, T, NT]), ALU.mult))
            for k in range(TOPK):
                for t in range(T):
                    v.tensor_scalar(onehot_s[:, k, t, :], iota_s[:, :], slot_f[:, 0, k, t:t + 1], None,
                                    ALU.is_equal).then_inc(told_done, 1)
            v.wait_ge(slots_full, 1)
            told_ps = pv_ps[0].rearrange("p u m -> p (u m)")[:, 0:PAY * NT].rearrange("p (c i) -> p c i", c=PAY)
            then(v.tensor_copy(tok[:, :], told_ps[:, 0, :]))
            then(v.tensor_copy(wlow[:, :], told_ps[:, 2, :]))
            then(v.scalar_tensor_tensor(wslot[:, :], told_ps[:, 1, :], 1.0, wlow[:, :], op0=ALU.mult, op1=ALU.add))
            then(v.tensor_scalar(wslot[:, :], wslot[:, :], 1.0 / WSCALE, None, ALU.mult))
            then(v.tensor_scalar(empty[:, :], tok[:, :], 0.0, dump[:, 0:1], ALU.is_equal, ALU.mult))
            then(v.scalar_tensor_tensor(row_of[:, :], tok[:, :], -1.0, empty[:, :], op0=ALU.add, op1=ALU.add))
            v.tensor_copy(tiles_i[0:1, 0:1], tiles_i[0:1, 0:1]).then_inc(slots_done, 1)

            def next_gather(sl):
                if sl.has(-2):
                    v.wait_ge(gx_in[sl.par], (sl.upto - 1) * 16)
                v.tensor_scalar(gidx[sl.par][:, :], tok[:, bass.ds(sl.t, 1)], float(ROW0 - 1), None,
                                ALU.add).then_inc(gidx_done, 1)

            next_gather(Slots(0, 0))
            next_gather(Slots(0, 1))

            def experts(sl):
                if sl.has(2):
                    next_gather(sl.at(2))
                if sl.has(0):
                    v.wait_ge(sil_done, sl.t + 1)
                    v.wait_ge(h1_full, sl.t + 1)
                    if sl.has(-2):
                        v.wait_ge(inter_turned, sl.t - 1)
                    v.tensor_tensor(inter[sl.par], sil[sl.par], flat(max_ps[sl.par][:, 1]), ALU.mult).then_inc(inter_done, 1)
                if sl.has(-1):
                    done = sl.at(-1)
                    v.wait_ge(y_full, done.t + 1)
                    if sl.has(-3):
                        v.wait_ge(y_out, (done.t - 1) * 16)
                    v.tensor_copy(sidx[done.par][:, :], row_of[:, bass.ds(done.t, 1)])
                    v.tensor_scalar(y_sb[done.par], pv_ps[done.par][:, 0, :], wslot[:, bass.ds(done.t, 1)], None,
                                    ALU.mult).then_inc(y_done, 1)

            run_slots(v, experts)

        @block.tensor
        def _(pe):
            def scores_max(n, st, p, par, first=False):
                if p == 0:
                    pe.wait_ge(qk_in[st.k], (st.third + 1) * 80)
                if not first:
                    pe.wait_ge(max_read, n - 1)
                for mt in range(2):
                    for h in range(2):
                        last = nc.tensor.matmul(max_ps[par][:, mt, h, :], lhsT=Q[st.k][0:KR, p, mt * P:(mt + 1) * P],
                                                rhs=K[st.k][0:KR, h, p, :], start=True, stop=True)
                last.then_inc(max_full, 1)

            def free_ring(n, first=False):
                if not first:
                    pe.wait_ge(ring_read, n - 1)

            def turn_max(u, i, n, first=False):
                free_ring(n, first)
                pe.wait_ge(mp_done, u + 1)
                for mt in range(2):
                    last = nc.tensor.transpose(ring_ps[i][0:MXR * 4, 0, 64 * mt:64 * mt + 64].bitcast(f16),
                                               mp[:, i, mt].rearrange("p h r j -> p (h r j)"), identh[:, :])
                last.then_inc(ring_full, 1)

            def turn_v(st, j, par, n):
                free_ring(n)
                if j == 0:
                    pe.wait_ge(v_in[st.par], st.half1 * 16)
                nc.tensor.transpose(ring_ps[par][:, 0, 0:P], v_sb[:, st.par, j * P:(j + 1) * P],
                                    ident[:, :]).then_inc(ring_full, 1)

            def turn_rows(m, par, n):
                free_ring(n)
                pe.wait_ge(ln2_done, m + 1)
                for u in range(2):
                    for k in range(KC):
                        last = nc.tensor.transpose(ring_ps[par][:, u, k * P:(k + 1) * P], normed[:, u, k * P:(k + 1) * P],
                                                   ident[:, :])
                last.then_inc(ring_full, 1)

            def logits(par, n, rows):
                free_ring(n)
                pe.wait_ge(ring_read, rows + 1)
                for u in range(2):
                    for k in range(KC):
                        last = nc.tensor.matmul(ring_ps[par][:, u, 0:E], lhsT=gT[:, 2 * u + k, :], rhs=gate_sb[:, k, :],
                                                start=(k == 0), stop=(k == KC - 1))
                last.then_inc(ring_full, 1)

            def scores_exp(st, e):
                p, h = e // 2, e % 2
                free_ring(ring(st, ("exp", e)))
                if e % 8 == 0:
                    pe.wait_ge(mrow_in[e // 8], (st.t + 1) * 16)
                for nt in range(2):
                    last = nc.tensor.matmul(bank(st, ("exp", e))[:, nt, :],
                                            lhsT=K[st.k][0:KR + MXR, h, p, nt * P:(nt + 1) * P],
                                            rhs=Q[st.k][:, p, :], start=True, stop=True)
                last.then_inc(ring_full, 1)

            def pv(st, q):
                pe.wait_ge(ring_read, ring(st, ("exp", 4 * q + 3)) + 1)
                if q % 2 == 0 and st.past(1):
                    pe.wait_ge(pv_read, st.t * 2 + (q // 2 - 1))
                for nt in range(2):
                    for j in range(4):
                        last = nc.tensor.matmul(pv_ps[q // 2][32 * j:32 * j + HD + 1, q % 2, :],
                                                lhsT=vT[st.k][:, nt, 4 * q + j, :], rhs=pt[:, (4 * q + j) % PTN, nt, :],
                                                start=(nt == 0), stop=(nt == 1))
                last.then_inc(pv_full, 1)

            pe.wait_ge(consts, 2)
            pe.wait_ge(fills, 1)
            for n in range(8):
                scores_max(n, Step(0, 0), n, n % 2, n < 2)
                if n == 6:
                    turn_max(0, 0, 0, True)
            scores_max(8, Step(0, 1), 0, 0)
            scores_max(9, Step(0, 1), 1, 1)
            turn_max(1, 1, 1, True)
            turn_v(Step(0, 0), 0, 0, 2)
            turn_v(Step(0, 0), 1, 1, 3)

            def step(st):
                for p in range(PAIRS):
                    if st.before(T - 2) or (st.before(T - 1) and p + LEAD < 2 * PAIRS):
                        scores_max(st.t * PAIRS + (p + LEAD), st.at((p + LEAD) // PAIRS), (p + LEAD) % PAIRS, p % 2)
                    if st.before(T - 1):
                        if p in (3, 7):
                            i = p // 4
                            turn_max(st.t * 2 + (2 + i), i, ring(st, ("max", i)))
                        if st.par == 0 and p == 4:
                            turn_rows(st.s, place(st, ("rows", 0)) % 2, ring(st, ("rows", 0)))
                        if st.par == 0 and p == 6:
                            logits(place(st, ("logits", 0)) % 2, ring(st, ("logits", 0)), ring(st, ("rows", 0)))
                        if p == 5:
                            for j in range(2):
                                turn_v(st.at(1), j, place(st, ("vt", j)) % 2, ring(st, ("vt", j)))
                    for h in range(2):
                        scores_exp(st, 2 * p + h)
                    if p % 2 == 0 and p > 0:
                        pv(st, p // 2 - 1)
                    if p == 0 and st.past(1):
                        pv(st.at(-1), 3)

            run_steps(pe, step)
            pv(Step(0, T - 1), 3)

            pe.wait_ge(max_read, T * PAIRS)
            pe.wait_ge(pv_read, T * 2)
            pe.wait_ge(ring_read, RING_END)
            for i in range(LAG):
                turn_rows(ST + i, 0, RING_END + 2 * i)
                logits(1, RING_END + 2 * i + 1, RING_END + 2 * i)
            pe.wait_ge(ring_read, RING_END + 2 * LAG)
            pe.wait_ge(w_in, W_LOADS * 16)
            pe.wait_ge(count_done, 1)
            pe.wait_ge(tables, 8)
            nc.tensor.matmul(pv_ps[1][:, 0, 0:E], lhsT=tri[:, :], rhs=rowcount[:, :], start=True, stop=True)
            nc.tensor.matmul(pv_ps[1][:, 0, E:2 * E], lhsT=ones[:, :], rhs=rowcount[:, :],
                             start=True, stop=True).then_inc(ranks_full, 1)
            for k in range(TOPK):
                for t in range(T):
                    n = k * T + t
                    pe.wait_ge(told_done, n + 1)
                    last = nc.tensor.matmul(pv_ps[0].rearrange("p u m -> p (u m)")[:, 0:PAY * NT]
                                            .rearrange("p (c i) -> p c i", c=PAY),
                                            lhsT=onehot_s[:, k, t, :], rhs=told[:, :, k, t, :],
                                            start=(n == 0), stop=(n == TOPK * T - 1))
            last.then_inc(slots_full, 1)

            def turn_x(sl):
                pe.wait_ge(gx_in[sl.par], sl.upto * 16)
                if sl.has(-1):
                    pe.wait_ge(xT_done, sl.t)
                for k in range(KC):
                    last = nc.tensor.transpose(ring_ps[1][:, 0, k * P:(k + 1) * P], gx[sl.par][:, k * P:(k + 1) * P],
                                               ident[:, :])
                last.then_inc(x_turned, 1)

            def turn_inter(sl):
                pe.wait_ge(inter_done, sl.t + 1)
                if sl.has(-1):
                    pe.wait_ge(interT_done, sl.t)
                for k in range(FC):
                    last = nc.tensor.transpose(flat(ring_ps[0])[:, k * P:(k + 1) * P], inter[sl.par][:, k * P:(k + 1) * P],
                                               ident[:, :])
                last.then_inc(inter_turned, 1)

            def expert(sl):
                return pe.value_load(expert_of[0:1, bass.ds(sl.t, 1)])

            def weight(w, e, n, k):
                return w[:, bass.ds(e * n + k, 1), :].rearrange("p o m -> p (o m)")

            def hidden(sl, e):
                pe.wait_ge(xT_done, sl.t + 1)
                if sl.has(-2):
                    pe.wait_ge(inter_done, sl.t - 1)
                for w, bank_of, full in ((w0_sb, 0, h0_full), (w1_sb, 1, h1_full)):
                    for k in range(KC):
                        last = nc.tensor.matmul(flat(max_ps[sl.par][:, bank_of]), lhsT=xT[sl.par][:, k * P:(k + 1) * P],
                                                rhs=weight(w, e, KC, k), start=(k == 0), stop=(k == KC - 1))
                    last.then_inc(full, 1)

            def output(sl, e):
                pe.wait_ge(interT_done, sl.t + 1)
                if sl.has(-2):
                    pe.wait_ge(y_done, sl.t - 1)
                for k in range(FC):
                    last = nc.tensor.matmul(pv_ps[sl.par][:, 0, :], lhsT=interT[sl.par][:, k * P:(k + 1) * P],
                                            rhs=weight(wo_sb, e, FC, k), start=(k == 0), stop=(k == FC - 1))
                last.then_inc(y_full, 1)

            pe.wait_ge(slots_done, 1)
            turn_x(Slots(0, 0))

            def experts(sl):
                e = expert(sl) if sl.has(0) else None
                e_before = expert(sl.at(-1)) if sl.has(-1) else None
                if sl.has(-1):
                    turn_inter(sl.at(-1))
                if sl.has(0):
                    hidden(sl, e)
                if sl.has(-1):
                    output(sl.at(-1), e_before)
                if sl.has(1):
                    turn_x(sl.at(1))

            run_slots(pe, experts)


def kernel(**inputs):
    import numpy as _np
    import concourse.bacc as _bacc
    from concourse import mybir as _mybir
    from concourse.bass_utils import run_bass_kernel_spmd as _run

    nc = _bacc.Bacc("TRN2", target_bir_lowering=False, num_devices=1)
    names = ["x", "ctx_2048", "L0_ffn_gate_kernel", "L0_ffn_w0_kernel", "L0_ffn_w1_kernel", "L0_ffn_wo_kernel"]
    arrays, args = {}, []
    for name in names:
        a = _np.ascontiguousarray(inputs[name])
        arrays[f"in_{name}"] = a
        args.append(nc.dram_tensor(f"in_{name}", a.shape, _mybir.dt.from_np(a.dtype), kind="ExternalInput").ap())
    shape = inputs["x"].shape
    args.append(nc.dram_tensor("out", shape, _mybir.dt.float32, kind="ExternalOutput").ap())
    xattn_ffn_kernel(nc, *args)
    r = _run(nc, [arrays], core_ids=[0])
    return r.results[0]["out"]
```
